# Optimizing a Trainium2 kernel written in Bass

```python
import numpy as np
import jax
import jax.numpy as jnp

def _softmax(x, axis=-1):
    return jax.nn.softmax(x, axis=axis)

def _gelu(x):
    return jax.nn.gelu(x, approximate=True)

def _silu(x):
    return jax.nn.silu(x)

def _sigmoid(x):
    return jax.nn.sigmoid(x)

def _layernorm(x, axis=-1, eps=1e-05):
    m = jnp.mean(x, axis=axis, keepdims=True)
    v = jnp.var(x, axis=axis, keepdims=True)
    return (x - m) / jnp.sqrt(v + eps)

def _scatter_add(tgt, idx, src, axis=0):
    return tgt.at[idx].add(src)

def _segment_sum(src, seg, n):
    return jax.ops.segment_sum(src, seg, n)
kernel_name = 'mk_flamingo_gated_d4_seqx_r8_634b9e'

def setup_inputs(seed: int=0):
    np.random.seed(seed)
    _w = jnp.asarray

    def _rec_inputs():
        import jax
        import jax.numpy as jnp
        _rk = jax.random.key(seed)
        x = -0.0005207 + 1.001 * jax.random.normal(jax.random.fold_in(_rk, 1), (8, 128, 512), jnp.float32)
        _lenS = 128 - jax.random.randint(jax.random.fold_in(_rk, 7), (8,), 0, max(1, 128 // 4) + 1, jnp.int32)
        _lenS2 = 128 - jax.random.randint(jax.random.fold_in(_rk, 8), (8,), 0, max(1, 128 // 4) + 1, jnp.int32)
        _ctx_4096P = jax.random.normal(jax.random.fold_in(_rk, 11), (8, 16, 512), jnp.float32)
        _ctx_4096c = jax.random.dirichlet(jax.random.fold_in(_rk, 511), 0.3 * jnp.ones((16,), jnp.float32), (8, 128))
        _ctx_4096t = jnp.einsum('bsk,bkd->bsd', _ctx_4096c, _ctx_4096P)
        _ctx_4096t = _ctx_4096t * jax.lax.rsqrt(jnp.mean(jnp.square(_ctx_4096t)) + 1e-12) * 0.953939
        ctx_4096 = -0.00010331 + 0.999899 * (_ctx_4096t + 0.3 * jax.random.normal(jax.random.fold_in(_rk, 611), (8, 128, 512), jnp.float32))
        pos_BxS2 = jnp.broadcast_to(jnp.arange(128, dtype=jnp.int32), (8, 128))
        _validS = jnp.arange(128)[None, :] < _lenS[:, None]
        _validS2 = jnp.arange(128)[None, :] < _lenS2[:, None]
        _causal = jnp.tril(jnp.ones((128, 128), dtype=bool))
        mask_BxSxS2_ik0 = jnp.where(jnp.broadcast_to(_validS2[:, None, :], (8, 128, 128)), 0, 1).astype(jnp.int32)
        _g = jax.random.normal(jax.random.fold_in(_rk, 9001), (2, 4), jnp.float32)
        _g = jnp.sign(_g) * jnp.maximum(jnp.abs(_g), 1.0) + (_g == 0) * 1.0
        g_xattn = _g[0]
        g_ffn = _g[1]
        return (x, ctx_4096, pos_BxS2, mask_BxSxS2_ik0, g_xattn, g_ffn)
    x, ctx_4096, pos_BxS2, mask_BxSxS2_ik0, g_xattn, g_ffn = _rec_inputs()

    def _L0_xattn_setup():
        import jax, jax.numpy as jnp
        import numpy as np
        B, Q, D = (8, 64, 512)
        CTX = 512
        H, KV, HD = (16, 4, 96)
        G = H // KV
        key = jax.random.key(seed)
        ks = jax.random.split(key, 6)
        s = 0.02
        return {'latents': jax.random.normal(ks[0], (B, Q, D), jnp.float32), 'context': jax.random.normal(ks[1], (B, CTX, D), jnp.float32), 'Wq': jax.random.normal(ks[2], (H * HD, D), jnp.float32) * s, 'Wk': jax.random.normal(ks[3], (KV * HD, D), jnp.float32) * s, 'Wv': jax.random.normal(ks[4], (KV * HD, D), jnp.float32) * s, 'Wo': jax.random.normal(ks[5], (D, H * HD), jnp.float32) * s}
    _L0_xattn_all = _L0_xattn_setup()
    _L0_xattn_in = {k: v for k, v in _L0_xattn_all.items() if k in ('Wq', 'Wk', 'Wv', 'Wo')}
    del _L0_xattn_all

    def _L0_ffn_setup():
        import jax, jax.numpy as jnp
        import numpy as np
        E = 8
        R = 8
        DIN = 512
        DOUT = 512
        TOP_K = 2
        SCALING = 2.0

        def _moe_lora(xf, gate_W, A, B):
            gate_probs = jax.nn.softmax(xf @ gate_W.T, axis=-1)
            weights, sel = jax.lax.top_k(gate_probs, TOP_K)
            weights = weights / jnp.sum(weights, axis=-1, keepdims=True)
            T = xf.shape[0]
            w_dense = jnp.zeros((T, E), xf.dtype).at[jnp.arange(T)[:, None], sel].add(weights)
            h = jnp.einsum('td,erd->ter', xf, A)
            h = h * (w_dense[:, :, None] * SCALING)
            return jnp.einsum('ter,eor->to', h, B)
        key = jax.random.key(seed)
        k0, k1, k2, k3, k4 = jax.random.split(key, 5)
        x = jax.random.normal(k0, (4, 256, DIN), jnp.float32)
        W_base = jax.random.normal(k1, (DOUT, DIN), jnp.float32) * 0.02
        gate_W = jax.random.normal(k2, (E, DIN), jnp.float32) * 0.02
        A = jax.random.normal(k3, (E, R, DIN), jnp.float32) * 0.02
        B = jax.random.normal(k4, (E, DOUT, R), jnp.float32) * 0.02
        return {'x': x, 'W_base': W_base, 'gate_W': gate_W, 'A': A, 'B': B}
    _L0_ffn_all = _L0_ffn_setup()
    _L0_ffn_in = {k: v for k, v in _L0_ffn_all.items() if k in ('W_base', 'gate_W', 'A', 'B')}
    del _L0_ffn_all

    def _L1_xattn_setup():
        import jax, jax.numpy as jnp
        import numpy as np
        EMB_DIM = 64
        HEADS = 8
        key = jax.random.key(seed)
        kq, kk, kv = jax.random.split(key, 3)
        B, C, N = (8, EMB_DIM, 512)
        q = jax.random.normal(kq, (B, C, N), dtype=jnp.float32)
        k = jax.random.normal(kk, (B, C, N), dtype=jnp.float32)
        v = jax.random.normal(kv, (B, C, N), dtype=jnp.float32)
        return {'q': q, 'k': k, 'v': v}
    _L1_xattn_all = _L1_xattn_setup()
    _L1_xattn_in = {k: v for k, v in _L1_xattn_all.items() if k in ()}
    del _L1_xattn_all

    def _L1_ffn_setup():
        import math
        import jax, jax.numpy as jnp
        import numpy as np
        SCALING = 16.0 / 32.0

        def real_fourier_orthogonal_multiply(c):
            n = c.shape[-1]
            sqrt_n = math.sqrt(n)
            pair_scale = math.sqrt(n / 2.0)
            max_f = (n - 1) // 2
            work = c.astype(jnp.float32)
            dc = (work[..., 0] * sqrt_n)[..., None].astype(jnp.complex64)
            cos = work[..., 1:1 + 2 * max_f:2] * pair_scale
            sin = work[..., 2:2 + 2 * max_f:2] * pair_scale
            mid = (cos - 1j * sin).astype(jnp.complex64)
            parts = [dc, mid]
            if n % 2 == 0:
                parts.append((work[..., -1] * sqrt_n)[..., None].astype(jnp.complex64))
            spectrum = jnp.concatenate(parts, axis=-1)
            return jnp.fft.irfft(spectrum, n=n, axis=-1).astype(c.dtype)
        key = jax.random.key(seed)
        ks = jax.random.split(key, 9)
        B, S, D_in, D_out, R0, R1, E = (4, 256, 512, 512, 32, 8, 3)
        x = jax.random.normal(ks[0], (B, S, D_in), dtype=jnp.float32)
        W_base = jax.random.normal(ks[1], (D_out, D_in), dtype=jnp.float32) * 0.02
        b_base = jax.random.normal(ks[2], (D_out,), dtype=jnp.float32) * 0.02
        enc0 = jax.random.normal(ks[3], (R0, D_in), dtype=jnp.float32) * 0.02
        enc1 = jax.random.normal(ks[4], (R1, D_in), dtype=jnp.float32) * 0.02
        coefs0 = jax.random.normal(ks[5], (E, D_out, R0), dtype=jnp.float32) * 0.02
        coefs1 = jax.random.normal(ks[6], (E, D_out, R1), dtype=jnp.float32) * 0.02
        mask0 = jax.random.randint(ks[7], (E, D_out, R0), 0, 2).astype(bool)
        mask1 = jax.random.randint(ks[8], (E, D_out, R1), 0, 2).astype(bool)
        return dict(x=x, W_base=W_base, b_base=b_base, enc0=enc0, enc1=enc1, coefs0=coefs0, coefs1=coefs1, mask0=mask0, mask1=mask1)
    _L1_ffn_all = _L1_ffn_setup()
    _L1_ffn_in = {k: v for k, v in _L1_ffn_all.items() if k in ('W_base', 'b_base', 'enc0', 'enc1', 'coefs0', 'coefs1', 'mask0', 'mask1')}
    del _L1_ffn_all

    def _L2_xattn_setup():
        import jax, jax.numpy as jnp
        import numpy as np
        B, S, E = (2, 256, 512)
        H, KVH, D = (32, 8, 128)
        GROUPS = H // KVH
        MAX_POS = 512
        ROPE_THETA = 10000.0

        def _rope_tables(max_pos, dim, theta):
            inv_freq = 1.0 / theta ** (jnp.arange(0, dim, 2, dtype=jnp.float32) / dim)
            t = jnp.arange(max_pos, dtype=jnp.float32)
            freqs = jnp.einsum('i,j->ij', t, inv_freq)
            emb = jnp.concatenate([freqs, freqs], axis=-1)
            return (jnp.cos(emb), jnp.sin(emb))

        def _rotate_half(x):
            x1, x2 = (x[..., :x.shape[-1] // 2], x[..., x.shape[-1] // 2:])
            return jnp.concatenate([-x2, x1], axis=-1)
        key = jax.random.key(seed)
        ks = jax.random.split(key, 8)
        scale_w = 1.0 / np.sqrt(E)
        query = jax.random.normal(ks[0], (B, S, E), dtype=jnp.float32)
        k_in = jax.random.normal(ks[1], (B, S, E), dtype=jnp.float32)
        v_in = jax.random.normal(ks[2], (B, S, E), dtype=jnp.float32)
        position_ids = jnp.broadcast_to(jnp.arange(S, dtype=jnp.int64), (B, S))
        src_mask = jnp.tril(jnp.ones((S, S), dtype=jnp.int32))
        src_mask = jnp.broadcast_to(src_mask, (B, S, S))
        Wq = jax.random.normal(ks[3], (E, H * D), dtype=jnp.float32) * scale_w
        Wk = jax.random.normal(ks[4], (E, KVH * D), dtype=jnp.float32) * scale_w
        Wv = jax.random.normal(ks[5], (E, KVH * D), dtype=jnp.float32) * scale_w
        Wo = jax.random.normal(ks[6], (H * D, E), dtype=jnp.float32) * scale_w
        return {'query': query, 'key': k_in, 'value': v_in, 'position_ids': position_ids, 'src_mask': src_mask, 'Wq': Wq, 'Wk': Wk, 'Wv': Wv, 'Wo': Wo}
    _L2_xattn_all = _L2_xattn_setup()
    _L2_xattn_in = {k: v for k, v in _L2_xattn_all.items() if k in ('Wq', 'Wk', 'Wv', 'Wo')}
    del _L2_xattn_all

    def _L2_ffn_setup():
        import jax, jax.numpy as jnp
        import numpy as np
        B, S, D, O, E, R = (2, 512, 512, 512, 8, 16)
        TOP_K = 2
        SCALING = 32.0 / 16.0
        key = jax.random.key(seed)
        k = jax.random.split(key, 6)
        x = jax.random.normal(k[0], (B, S, D), dtype=jnp.float32)
        W_base = jax.random.normal(k[1], (O, D), dtype=jnp.float32) * 0.02
        b_base = jax.random.normal(k[2], (O,), dtype=jnp.float32) * 0.02
        W_router = jax.random.normal(k[3], (E, D), dtype=jnp.float32) * 0.01
        lora_A = jax.random.normal(k[4], (E, R, D), dtype=jnp.float32) * (1.0 / np.sqrt(D))
        lora_B = jax.random.normal(k[5], (E, O, R), dtype=jnp.float32) * 0.02
        return {'x': x, 'W_base': W_base, 'b_base': b_base, 'W_router': W_router, 'lora_A': lora_A, 'lora_B': lora_B}
    _L2_ffn_all = _L2_ffn_setup()
    _L2_ffn_in = {k: v for k, v in _L2_ffn_all.items() if k in ('W_base', 'b_base', 'W_router', 'lora_A', 'lora_B')}
    del _L2_ffn_all

    def _L3_xattn_setup():
        import jax, jax.numpy as jnp
        import numpy as np
        EMB_DIM = 512
        NHEADS = 32
        KVHEADS = 8
        HEAD_DIM = 128
        ROPE_BASE = 10000.0

        def _rope(x):
            B, H, S, D = x.shape
            inv_freq = 1.0 / ROPE_BASE ** (jnp.arange(0, D, 2, dtype=jnp.float32) / D)
            ang = jnp.arange(S, dtype=jnp.float32)[:, None] * inv_freq[None, :]
            cos = jnp.concatenate([jnp.cos(ang), jnp.cos(ang)], axis=-1)
            sin = jnp.concatenate([jnp.sin(ang), jnp.sin(ang)], axis=-1)
            x1, x2 = (x[..., :D // 2], x[..., D // 2:])
            rot = jnp.concatenate([-x2, x1], axis=-1)
            return x * cos + rot * sin
        key = jax.random.key(seed)
        ks = jax.random.split(key, 7)
        B, S = (2, 256)
        std_qk = EMB_DIM ** (-0.5)
        std_vd = (1.0 / (EMB_DIM * NHEADS * HEAD_DIM) ** 0.5) ** 0.5
        return {'q': jax.random.normal(ks[0], (B, S, EMB_DIM), jnp.float32), 'k': jax.random.normal(ks[1], (B, S, EMB_DIM), jnp.float32), 'v': jax.random.normal(ks[2], (B, S, EMB_DIM), jnp.float32), 'Wq': jax.random.normal(ks[3], (NHEADS * HEAD_DIM, EMB_DIM), jnp.float32) * std_qk, 'Wk': jax.random.normal(ks[4], (KVHEADS * HEAD_DIM, EMB_DIM), jnp.float32) * std_qk, 'Wv': jax.random.normal(ks[5], (KVHEADS * HEAD_DIM, EMB_DIM), jnp.float32) * std_vd, 'Wd': jax.random.normal(ks[6], (EMB_DIM, NHEADS * HEAD_DIM), jnp.float32) * std_vd}
    _L3_xattn_all = _L3_xattn_setup()
    _L3_xattn_in = {k: v for k, v in _L3_xattn_all.items() if k in ('Wq', 'Wk', 'Wv', 'Wd')}
    del _L3_xattn_all

    def _L3_ffn_setup():
        import jax, jax.numpy as jnp
        import numpy as np
        B, S, D, O, E, R = (4, 256, 512, 512, 8, 16)
        SCALING = 32.0 / 16.0
        MAX_THRESHOLD = 0.125
        key = jax.random.key(seed)
        ks = jax.random.split(key, 8)
        return {'x': jax.random.normal(ks[0], (B, S, D), jnp.float32), 'W_base': jax.random.normal(ks[1], (O, D), jnp.float32) * (1.0 / np.sqrt(D)), 'b_base': jax.random.normal(ks[2], (O,), jnp.float32) * 0.02, 'W_gate': jax.random.normal(ks[3], (E, D), jnp.float32) * (1.0 / np.sqrt(D)), 'W_thr': jax.random.normal(ks[4], (D,), jnp.float32) * (1.0 / np.sqrt(D)), 'b_thr': jax.random.normal(ks[5], (1,), jnp.float32) * 0.02, 'A_w': jax.random.normal(ks[6], (E, R, D), jnp.float32) * (1.0 / np.sqrt(D)), 'B_w': jax.random.normal(ks[7], (E, O, R), jnp.float32) * (1.0 / np.sqrt(R))}
    _L3_ffn_all = _L3_ffn_setup()
    _L3_ffn_in = {k: v for k, v in _L3_ffn_all.items() if k in ('W_base', 'b_base', 'W_gate', 'W_thr', 'b_thr', 'A_w', 'B_w')}
    del _L3_ffn_all
    return {'x': x, 'ctx_4096': ctx_4096, 'pos_BxS2': pos_BxS2, 'mask_BxSxS2_ik0': mask_BxSxS2_ik0, 'g_xattn': g_xattn, 'g_ffn': g_ffn, 'L0_xattn_Wq': _L0_xattn_in['Wq'], 'L0_xattn_Wk': _L0_xattn_in['Wk'], 'L0_xattn_Wv': _L0_xattn_in['Wv'], 'L0_xattn_Wo': _L0_xattn_in['Wo'], 'L0_ffn_W_base': _L0_ffn_in['W_base'], 'L0_ffn_gate_W': _L0_ffn_in['gate_W'], 'L0_ffn_A': _L0_ffn_in['A'], 'L0_ffn_B': _L0_ffn_in['B'], 'L1_ffn_W_base': _L1_ffn_in['W_base'], 'L1_ffn_b_base': _L1_ffn_in['b_base'], 'L1_ffn_enc0': _L1_ffn_in['enc0'], 'L1_ffn_enc1': _L1_ffn_in['enc1'], 'L1_ffn_coefs0': _L1_ffn_in['coefs0'], 'L1_ffn_coefs1': _L1_ffn_in['coefs1'], 'L1_ffn_mask0': _L1_ffn_in['mask0'], 'L1_ffn_mask1': _L1_ffn_in['mask1'], 'L2_xattn_Wq': _L2_xattn_in['Wq'], 'L2_xattn_Wk': _L2_xattn_in['Wk'], 'L2_xattn_Wv': _L2_xattn_in['Wv'], 'L2_xattn_Wo': _L2_xattn_in['Wo'], 'L2_ffn_W_base': _L2_ffn_in['W_base'], 'L2_ffn_b_base': _L2_ffn_in['b_base'], 'L2_ffn_W_router': _L2_ffn_in['W_router'], 'L2_ffn_lora_A': _L2_ffn_in['lora_A'], 'L2_ffn_lora_B': _L2_ffn_in['lora_B'], 'L3_xattn_Wq': _L3_xattn_in['Wq'], 'L3_xattn_Wk': _L3_xattn_in['Wk'], 'L3_xattn_Wv': _L3_xattn_in['Wv'], 'L3_xattn_Wd': _L3_xattn_in['Wd'], 'L3_ffn_W_base': _L3_ffn_in['W_base'], 'L3_ffn_b_base': _L3_ffn_in['b_base'], 'L3_ffn_W_gate': _L3_ffn_in['W_gate'], 'L3_ffn_W_thr': _L3_ffn_in['W_thr'], 'L3_ffn_b_thr': _L3_ffn_in['b_thr'], 'L3_ffn_A_w': _L3_ffn_in['A_w'], 'L3_ffn_B_w': _L3_ffn_in['B_w']}

def reference(x, ctx_4096, pos_BxS2, mask_BxSxS2_ik0, g_xattn, g_ffn, L0_xattn_Wq, L0_xattn_Wk, L0_xattn_Wv, L0_xattn_Wo, L0_ffn_W_base, L0_ffn_gate_W, L0_ffn_A, L0_ffn_B, L1_ffn_W_base, L1_ffn_b_base, L1_ffn_enc0, L1_ffn_enc1, L1_ffn_coefs0, L1_ffn_coefs1, L1_ffn_mask0, L1_ffn_mask1, L2_xattn_Wq, L2_xattn_Wk, L2_xattn_Wv, L2_xattn_Wo, L2_ffn_W_base, L2_ffn_b_base, L2_ffn_W_router, L2_ffn_lora_A, L2_ffn_lora_B, L3_xattn_Wq, L3_xattn_Wk, L3_xattn_Wv, L3_xattn_Wd, L3_ffn_W_base, L3_ffn_b_base, L3_ffn_W_gate, L3_ffn_W_thr, L3_ffn_b_thr, L3_ffn_A_w, L3_ffn_B_w):
    import jax
    import jax.numpy as jnp

    def _L0_xattn_ref(latents, context, Wq, Wk, Wv, Wo):
        import jax, jax.numpy as jnp
        import numpy as np
        B, Q, D = (8, 64, 512)
        CTX = 512
        H, KV, HD = (16, 4, 96)
        G = H // KV
        b, q_len, _ = latents.shape
        hidden = jnp.concatenate([context, latents], axis=1)
        s_len = hidden.shape[1]
        q = (latents @ Wq.T).reshape(b, q_len, H, HD)
        k = (hidden @ Wk.T).reshape(b, s_len, KV, HD)
        v = (hidden @ Wv.T).reshape(b, s_len, KV, HD)
        q = q.transpose(0, 2, 1, 3).reshape(b, KV, G, q_len, HD)
        k = k.transpose(0, 2, 1, 3)
        v = v.transpose(0, 2, 1, 3)
        scale = 1.0 / jnp.sqrt(jnp.asarray(HD, q.dtype))
        scores = jnp.einsum('bkgqd,bksd->bkgqs', q, k) * scale
        attn = jax.nn.softmax(scores.astype(jnp.float32), axis=-1).astype(q.dtype)
        out = jnp.einsum('bkgqs,bksd->bkgqd', attn, v)
        out = out.reshape(b, H, q_len, HD).transpose(0, 2, 1, 3).reshape(b, q_len, H * HD)
        return out @ Wo.T

    def _L0_ffn_ref(x, W_base, gate_W, A, B):
        import jax, jax.numpy as jnp
        import numpy as np
        E = 8
        R = 8
        DIN = 512
        DOUT = 512
        TOP_K = 2
        SCALING = 2.0

        def _moe_lora(xf, gate_W, A, B):
            gate_probs = jax.nn.softmax(xf @ gate_W.T, axis=-1)
            weights, sel = jax.lax.top_k(gate_probs, TOP_K)
            weights = weights / jnp.sum(weights, axis=-1, keepdims=True)
            T = xf.shape[0]
            w_dense = jnp.zeros((T, E), xf.dtype).at[jnp.arange(T)[:, None], sel].add(weights)
            h = jnp.einsum('td,erd->ter', xf, A)
            h = h * (w_dense[:, :, None] * SCALING)
            return jnp.einsum('ter,eor->to', h, B)
        xf = x.reshape(-1, x.shape[-1])
        out = xf @ W_base.T + _moe_lora(xf, gate_W, A, B)
        return out.reshape(*x.shape[:-1], DOUT)

    def _L1_xattn_ref(q, k, v):
        import jax, jax.numpy as jnp
        import numpy as np
        EMB_DIM = 64
        HEADS = 8
        B, C, N = q.shape
        H = HEADS
        dh = C // H
        qh = q.transpose(0, 2, 1).reshape(B, N, H, dh)
        kh = k.transpose(0, 2, 1).reshape(B, N, H, dh)
        vh = v.transpose(0, 2, 1).reshape(B, N, H, dh)
        qh = jax.nn.softmax(qh, axis=3)
        kh = jax.nn.softmax(kh, axis=1)
        kvs = jnp.einsum('bnhd,bnhe->bhde', kh, vh)
        out = jnp.einsum('bnhd,bhde->bnhe', qh, kvs)
        return out.transpose(0, 2, 3, 1).reshape(B, C, N)

    def _L1_ffn_ref(x, W_base, b_base, enc0, enc1, coefs0, coefs1, mask0, mask1):
        import math
        import jax, jax.numpy as jnp
        import numpy as np
        SCALING = 16.0 / 32.0

        def real_fourier_orthogonal_multiply(c):
            n = c.shape[-1]
            sqrt_n = math.sqrt(n)
            pair_scale = math.sqrt(n / 2.0)
            max_f = (n - 1) // 2
            work = c.astype(jnp.float32)
            dc = (work[..., 0] * sqrt_n)[..., None].astype(jnp.complex64)
            cos = work[..., 1:1 + 2 * max_f:2] * pair_scale
            sin = work[..., 2:2 + 2 * max_f:2] * pair_scale
            mid = (cos - 1j * sin).astype(jnp.complex64)
            parts = [dc, mid]
            if n % 2 == 0:
                parts.append((work[..., -1] * sqrt_n)[..., None].astype(jnp.complex64))
            spectrum = jnp.concatenate(parts, axis=-1)
            return jnp.fft.irfft(spectrum, n=n, axis=-1).astype(c.dtype)
        base = jnp.einsum('bsd,od->bso', x, W_base) + b_base
        e0 = jnp.einsum('bsd,rd->bsr', x, enc0)
        e1 = jnp.einsum('bsd,rd->bsr', x, enc1)
        w0 = coefs0 * mask0.astype(coefs0.dtype)
        w1 = coefs1 * mask1.astype(coefs1.dtype)
        decoded = jnp.einsum('bsr,eor->ebso', e0, w0) + jnp.einsum('bsr,eor->ebso', e1, w1)
        transformed = real_fourier_orthogonal_multiply(decoded)
        update = transformed.sum(axis=0)
        return base + update * SCALING

    def _L2_xattn_ref(query, key, value, position_ids, src_mask, Wq, Wk, Wv, Wo):
        import jax, jax.numpy as jnp
        import numpy as np
        B, S, E = (2, 256, 512)
        H, KVH, D = (32, 8, 128)
        GROUPS = H // KVH
        MAX_POS = 512
        ROPE_THETA = 10000.0

        def _rope_tables(max_pos, dim, theta):
            inv_freq = 1.0 / theta ** (jnp.arange(0, dim, 2, dtype=jnp.float32) / dim)
            t = jnp.arange(max_pos, dtype=jnp.float32)
            freqs = jnp.einsum('i,j->ij', t, inv_freq)
            emb = jnp.concatenate([freqs, freqs], axis=-1)
            return (jnp.cos(emb), jnp.sin(emb))

        def _rotate_half(x):
            x1, x2 = (x[..., :x.shape[-1] // 2], x[..., x.shape[-1] // 2:])
            return jnp.concatenate([-x2, x1], axis=-1)
        nb, q_len, _ = query.shape
        q = (query @ Wq).reshape(nb, q_len, H, D).transpose(0, 2, 1, 3)
        k = (key @ Wk).reshape(nb, q_len, KVH, D).transpose(0, 2, 1, 3)
        v = (value @ Wv).reshape(nb, q_len, KVH, D).transpose(0, 2, 1, 3)
        cos_t, sin_t = _rope_tables(MAX_POS, D, ROPE_THETA)
        cos = cos_t[position_ids][:, None]
        sin = sin_t[position_ids][:, None]
        q = q * cos + _rotate_half(q) * sin
        k = k * cos + _rotate_half(k) * sin
        k = jnp.repeat(k, GROUPS, axis=1)
        v = jnp.repeat(v, GROUPS, axis=1)
        scores = jnp.einsum('bhqd,bhkd->bhqk', q, k) / jnp.sqrt(jnp.float32(D))
        mask = src_mask[:, None]
        scores = jnp.where(mask == 0, jnp.float32(-1000000000.0), scores)
        attn = jax.nn.softmax(scores, axis=-1)
        x = jnp.einsum('bhqk,bhkd->bhqd', attn, v)
        x = x.transpose(0, 2, 1, 3).reshape(nb, q_len, H * D)
        return x @ Wo

    def _L2_ffn_ref(x, W_base, b_base, W_router, lora_A, lora_B):
        import jax, jax.numpy as jnp
        import numpy as np
        B, S, D, O, E, R = (2, 512, 512, 512, 8, 16)
        TOP_K = 2
        SCALING = 32.0 / 16.0
        d = x.shape[-1]
        n_experts = W_router.shape[0]
        xf = x.reshape(-1, d)
        logits = xf @ W_router.T
        probs = jax.nn.softmax(logits, axis=-1)
        topk_p, topk_i = jax.lax.top_k(probs, TOP_K)
        topk_p = topk_p / jnp.sum(topk_p, axis=-1, keepdims=True)
        w = jnp.sum(jax.nn.one_hot(topk_i, n_experts, dtype=xf.dtype) * topk_p[..., None], axis=1)
        h = jnp.einsum('td,erd->ter', xf, lora_A)
        lora_out = jnp.einsum('ter,eor,te->to', h, lora_B, w) * SCALING
        base = x @ W_base.T + b_base
        return base + lora_out.reshape(x.shape[:-1] + (W_base.shape[0],))

    def _L3_xattn_ref(q, k, v, Wq, Wk, Wv, Wd):
        import jax, jax.numpy as jnp
        import numpy as np
        EMB_DIM = 512
        NHEADS = 32
        KVHEADS = 8
        HEAD_DIM = 128
        ROPE_BASE = 10000.0

        def _rope(x):
            B, H, S, D = x.shape
            inv_freq = 1.0 / ROPE_BASE ** (jnp.arange(0, D, 2, dtype=jnp.float32) / D)
            ang = jnp.arange(S, dtype=jnp.float32)[:, None] * inv_freq[None, :]
            cos = jnp.concatenate([jnp.cos(ang), jnp.cos(ang)], axis=-1)
            sin = jnp.concatenate([jnp.sin(ang), jnp.sin(ang)], axis=-1)
            x1, x2 = (x[..., :D // 2], x[..., D // 2:])
            rot = jnp.concatenate([-x2, x1], axis=-1)
            return x * cos + rot * sin
        B, Sq, _ = q.shape
        Skv = k.shape[1]
        queries = (q @ Wq.T).reshape(B, Sq, NHEADS, HEAD_DIM).transpose(0, 2, 1, 3)
        keys = (k @ Wk.T).reshape(B, Skv, KVHEADS, HEAD_DIM).transpose(0, 2, 1, 3)
        values = (v @ Wv.T).reshape(B, Skv, KVHEADS, HEAD_DIM).transpose(0, 2, 1, 3)
        queries = _rope(queries)
        keys = _rope(keys)
        exp = NHEADS // KVHEADS
        keys = jnp.repeat(keys, exp, axis=1)
        values = jnp.repeat(values, exp, axis=1)
        scale = HEAD_DIM ** (-0.5)
        scores = jnp.einsum('bhqd,bhkd->bhqk', queries, keys) * scale
        causal = jnp.tril(jnp.ones((Sq, Skv), dtype=bool))
        scores = jnp.where(causal[None, None], scores, jnp.finfo(scores.dtype).min)
        attn = jax.nn.softmax(scores, axis=-1)
        ctx = jnp.einsum('bhqk,bhkd->bhqd', attn, values)
        ctx = ctx.transpose(0, 2, 1, 3).reshape(B, Sq, NHEADS * HEAD_DIM)
        return ctx @ Wd.T

    def _L3_ffn_ref(x, W_base, b_base, W_gate, W_thr, b_thr, A_w, B_w):
        import jax, jax.numpy as jnp
        import numpy as np
        B, S, D, O, E, R = (4, 256, 512, 512, 8, 16)
        SCALING = 32.0 / 16.0
        MAX_THRESHOLD = 0.125
        base = jnp.einsum('bsd,od->bso', x, W_base) + b_base
        xf = x.reshape(-1, D)
        gate = jax.nn.softmax(xf @ W_gate.T, axis=-1)
        thr = jax.nn.sigmoid(xf @ W_thr + b_thr[0]) * MAX_THRESHOLD
        adapted = gate - thr[:, None]
        selected = (adapted >= 0).astype(x.dtype)
        w = adapted * selected
        wsum = jnp.sum(w, axis=-1, keepdims=True)
        wsum = jnp.where(wsum == 0, jnp.ones_like(wsum), wsum)
        w = w / wsum
        h = jnp.einsum('nd,erd->ner', xf, A_w)
        moe = jnp.einsum('ner,ne,eor->no', h, w, B_w) * SCALING
        return base + moe.reshape(base.shape)
    x = x + jnp.tanh(g_xattn[0]) * _L0_xattn_ref(_layernorm(x, axis=-1), ctx_4096, L0_xattn_Wq, L0_xattn_Wk, L0_xattn_Wv, L0_xattn_Wo)
    x = x + jnp.tanh(g_ffn[0]) * _L0_ffn_ref(_layernorm(x, axis=-1), L0_ffn_W_base, L0_ffn_gate_W, L0_ffn_A, L0_ffn_B)
    x = x + jnp.tanh(g_xattn[1]) * _L1_xattn_ref(_layernorm(x, axis=-1), ctx_4096, ctx_4096)
    x = x + jnp.tanh(g_ffn[1]) * _L1_ffn_ref(_layernorm(x, axis=-1), L1_ffn_W_base, L1_ffn_b_base, L1_ffn_enc0, L1_ffn_enc1, L1_ffn_coefs0, L1_ffn_coefs1, L1_ffn_mask0, L1_ffn_mask1)
    x = x + jnp.tanh(g_xattn[2]) * _L2_xattn_ref(_layernorm(x, axis=-1), ctx_4096, ctx_4096, pos_BxS2, mask_BxSxS2_ik0, L2_xattn_Wq, L2_xattn_Wk, L2_xattn_Wv, L2_xattn_Wo)
    x = x + jnp.tanh(g_ffn[2]) * _L2_ffn_ref(_layernorm(x, axis=-1), L2_ffn_W_base, L2_ffn_b_base, L2_ffn_W_router, L2_ffn_lora_A, L2_ffn_lora_B)
    x = x + jnp.tanh(g_xattn[3]) * _L3_xattn_ref(_layernorm(x, axis=-1), ctx_4096, ctx_4096, L3_xattn_Wq, L3_xattn_Wk, L3_xattn_Wv, L3_xattn_Wd)
    x = x + jnp.tanh(g_ffn[3]) * _L3_ffn_ref(_layernorm(x, axis=-1), L3_ffn_W_base, L3_ffn_b_base, L3_ffn_W_gate, L3_ffn_W_thr, L3_ffn_b_thr, L3_ffn_A_w, L3_ffn_B_w)
    return x

_drawn_inputs = setup_inputs


def setup_inputs(seed=0):
    import zlib

    import numpy as np

    out = dict(_drawn_inputs(seed))
    spreads = {}
    factors = {'L0_xattn_Wq': 7.888,
     'L0_xattn_Wk': 7.635,
     'L1_ffn_b_base': 4.065,
     'L1_ffn_enc1': 4.801,
     'L1_ffn_coefs1': 4.865,
     'L2_ffn_b_base': 6.125,
     'L3_ffn_b_base': 7.106,
     'L0_ffn_gate_W': 2.865,
     'L1_ffn_enc0': 2.671}
    for name, (base, spread) in spreads.items():
        noise = np.random.default_rng([zlib.crc32(name.encode()), seed]).standard_normal(out[name].shape)
        drawn = base * np.exp(spread * noise) if base else spread * noise
        out[name] = jnp.asarray(drawn.astype(out[name].dtype))
    for name, factor in factors.items():
        out[name] = (out[name] * factor).astype(out[name].dtype)
    return out
```

```python
from contextlib import ExitStack

import numpy as np

import concourse.bass as bass
from concourse import mybir
from concourse.alu_op_type import AluOpType as ALU

F32 = mybir.dt.float32
F32R = mybir.dt.float32r
I32 = mybir.dt.int32
U8 = mybir.dt.uint8
ACT = mybir.ActivationFunctionType
X_AXIS = mybir.AxisListType.X

B, P, D = 8, 128, 512
T = B * P
C = D // P
HALF = 4
GH = 4
NE = 8
RAW = 5
RAW_COLS = C * (P + NE + 2)
LN_EPS = 1e-5

FILL_ROPE = {3: [("K", 0), ("Q", 0)], 4: [("V", 0), ("Q", 1)], 5: [("Q", 2)], 6: [("Q", 3)]}
FILL_TWO = {3: [("K", 0), ("Q", 0)], 4: [("V", 0), ("Q", 1)], 5: [("K", 1), ("Q", 2)], 6: [("V", 1), ("Q", 3)]}
WEIGHT_ORDER = {("Q", 0): 0, "K": 1, ("Q", 1): 2, "V": 3, ("Q", 2): 4, ("Q", 3): 5}
SPLIT_AT = {1: [0], 2: [1, 2], 3: [3, 4], 4: [5]}


PROLOGUE, NOW, BEFORE = range(3)


class Layer:

    def __init__(self, name, groups, hd, sources, rope, gate):
        self.name, self.groups, self.hd, self.sources, self.rope, self.gate = name, groups, hd, sources, rope, gate
        fill = FILL_TWO if sources == 2 else FILL_ROPE
        self.fill = {b: fill[b if 3 <= b <= 6 else (b - 4) % 8] for b in range(8)}
        self.half = {b: 0 if 3 <= b <= 6 else 1 for b in range(8)}
        self.scale = float(hd) ** -0.5
        self.keys = sources * P
        self.weight_tiles = 10 * groups
        self.first = {b: sum(len(self.fill[k]) for k in range(3, b)) for b in range(3, 9)}
        self.off = {b: self.first[8] + sum(len(self.fill[k]) for k in range(b)) for b in range(8)}
        self.per_group = sum(len(f) for f in self.fill.values())

    def kinds(self, want, b, pro):
        n = lambda k: sum(1 for kind, _ in self.fill[k] if kind in want)
        if pro:
            return sum(n(k) for k in range(3, b))
        return sum(n(k) for k in range(3, 8)) + sum(n(k) for k in range(b))

    def kinds_group(self, want):
        return sum(1 for f in self.fill.values() for kind, _ in f if kind in want)

    def index(self, want, g, b, k, when=NOW):
        inside = sum(1 for kind, _ in self.fill[b][:k] if kind in want)
        base = self.kinds(want, b, when != NOW) + inside
        return base if when == PROLOGUE else self.kinds_group(want) * g + base

    def tile(self, g, b, k, when=NOW):
        base = (self.off[b] if when == NOW else self.first[b]) + k
        return (base if when == PROLOGUE else self.per_group * g + base), base % 2

    def two_before(self, b, k, when):
        steps = range(3, 8) if when == PROLOGUE else range(8)
        seq = [(s, j) for s in steps for j in range(len(self.fill[s]))]
        n = seq.index((b, k)) - 2
        if n >= 0:
            return seq[n] + (when,)
        if when == PROLOGUE:
            return None
        seq = [(s, j) for s in range(3, 8) for j in range(len(self.fill[s]))]
        return seq[n] + (BEFORE,)

    def ready(self, want, g, half):
        if half == 1:
            return g * self.kinds_group(want) + self.kinds(want, 3, False)
        return g * self.kinds_group(want) + self.kinds(want, 7, True)


def build(nc, inp, out):
    ctx = ExitStack()
    with ctx:
        sem = lambda name: ctx.enter_context(nc.semaphore(name))

        cursor = [384]

        def region(size):
            at = cursor[0]
            cursor[0] += (size + 31) // 32 * 32
            return at

        def at(name, shape, dt, offset):
            return nc.alloc_sbuf_tensor_at(name, shape, dt, offset=offset)

        def new(name, shape, dt):
            size = int(np.prod(shape[1:])) * (1 if dt == U8 else 4)
            return at(name, shape, dt, region(size))

        x = new("x", [P, B, D], F32)
        xt_hi = new("xt_hi", [P, C, T], F32R)
        xt_lo = new("xt_lo", [P, C, T], F32R)
        ct_hi = new("ct_hi", [P, C, T], F32R)
        ct_lo = new("ct_lo", [P, C, T], F32R)
        r_wq, r_wkv, r_wo = region(16384), region(8192), region(16384)
        r_q, r_k, r_v, r_pt = region(32768), region(16384), region(12288), region(10240)
        raw = new("raw", [P, RAW, RAW_COLS], F32)
        probs = new("probs", [P, GH * 2 * P], F32)
        ot_hi = new("ot_hi", [P, GH * P], F32R)
        ot_lo = new("ot_lo", [P, GH * P], F32R)
        xn = new("xn", [P, 2, D], F32)
        bias = new("bias", [P, D], F32)
        consts = new("consts", [P, 2 * P + NE + C], F32)
        ident, blk = consts[:, 0:P], consts[:, P:2 * P]
        iota8, pidx = consts[:, 2 * P:2 * P + NE], consts[:, 2 * P + NE:]
        blk_r = new("blk_r", [P, P], F32R)
        gates = new("gates", [P, 8], F32)
        tg = new("tg", [P, 8], F32)
        stats = new("stats", [P, 2, 6], F32)
        mv = new("mv", [P, 2, 2], F32)
        ve = new("ve", [P, 2], F32)
        rstd = new("rstd", [P, 2], F32)
        minus_half = new("minus_half", [P, 1], F32)
        fill = new("fill", [P, 2], F32)
        negmax = new("negmax", [P, 2, GH], F32)
        nbias = new("nbias", [P, 2, GH], F32)
        sums = new("sums", [P, 2, GH], F32)
        rsums = new("rsums", [P, 2, GH], F32)
        gt = new("gt", [P, 16, NE], F32)
        thr = new("thr", [P, 8], F32)
        bthr = new("bthr", [P, 1], F32)
        assert cursor[0] <= nc.sbuf_usable_end, cursor[0]

        Lq = [Layer("L0", 4, 96, 2, False, 0), Layer("L2", 8, 128, 1, True, 4), Layer("L3", 8, 128, 1, True, 6)]
        for L in Lq:
            n, hd, s = L.name, L.hd, L.sources
            kv = B * s * P * 4
            vb = B * s * hd * 4
            L.wq_hi = at(f"wq_hi{n}", [P, GH, C, hd], F32R, r_wq)
            L.wq_lo = at(f"wq_lo{n}", [P, GH, C, hd], F32R, r_wq + 8192)
            L.wkv_hi = at(f"wkv_hi{n}", [P, 2, C, hd], F32R, r_wkv)
            L.wkv_lo = at(f"wkv_lo{n}", [P, 2, C, hd], F32R, r_wkv + 4096)
            L.wo_hi = at(f"wo_hi{n}", [P, GH, D], F32R, r_wo)
            L.wo_lo = at(f"wo_lo{n}", [P, GH, D], F32R, r_wo + 8192)
            L.q_hi = at(f"q_hi{n}", [P, GH, T], F32R, r_q)
            L.q_lo = at(f"q_lo{n}", [P, GH, T], F32R, r_q + 16384)
            L.k_hi = at(f"k_hi{n}", [P, B, s, P], F32R, r_k)
            L.k_lo = at(f"k_lo{n}", [P, B, s, P], F32R, r_k + kv)
            L.v_hi = at(f"v_hi{n}", [P, B, s, hd], F32R, r_v)
            L.v_lo = at(f"v_lo{n}", [P, B, s, hd], F32R, r_v + vb)
            L.pt_hi = at(f"pt_hi{n}", [P, s, GH * P], F32R, r_pt)
            L.pt_lo = at(f"pt_lo{n}", [P, s, GH * P], F32R, r_pt + s * 2048)
        rope_a = at("rope_a", [P, 2, D], F32, r_pt + 4096)
        rope_b = at("rope_b", [P, D], F32, r_pt + 8192)
        cos2 = at("cos2", [P, T], F32, r_k + 8192)
        sin2 = at("sin2", [P, T], F32, r_k + 12288)
        rot3 = at("rot3", [P, 2, P], F32, r_k + 8192)
        mask2 = at("mask2", [P, B, P], U8, r_v + 8192)
        mask3 = at("mask3", [P, 1, P], U8, r_v + 8192 + 1024)
        causal = at("causal", [P, P], F32, r_v + 8192 + 1280)
        mask_in = at("mask_in", [P, B, P], I32, r_v)
        wt_hi = at("wt_hi", [P, C, D], F32R, r_wq)
        wt_lo = at("wt_lo", [P, C, D], F32R, r_wq + 8192)
        FF = []
        for f, er, extra in ((0, 64, 0), (1, 0, 0), (2, 128, 0), (3, 128, 2)):
            n = er + NE + extra
            FF.append(dict(
                f=f, er=er, cols=n,
                ag_hi=at(f"ag_hi{f}", [P, C, n], F32R, r_q) if er else None,
                ag_lo=at(f"ag_lo{f}", [P, C, n], F32R, r_q + 2304) if er else None,
                lb_hi=at(f"lb_hi{f}", [P, D], F32R, r_q + 4608) if er else None,
                lb_lo=at(f"lb_lo{f}", [P, D], F32R, r_q + 6656) if er else None))
        hw = at("hw", [P, 2, P], F32, r_q + 8704)
        hwt_hi = at("hwt_hi", [P, P], F32R, r_q + 9728)
        hwt_lo = at("hwt_lo", [P, P], F32R, r_q + 10240)
        ct_raw = at("ct_raw", [P, C, T], F32, r_q + 16384)
        cn_raw = at("cn_raw", [P, B, D], F32, r_q + 16384)
        kt_hi = at("kt_hi", [P, C, P], F32R, r_pt)
        kt_lo = at("kt_lo", [P, C, P], F32R, r_pt + 2048)
        kvs = at("kvs", [P, P], F32, r_pt + 4096)
        kvs_hi = at("kvs_hi", [P, B, P], F32R, r_k)
        kvs_lo = at("kvs_lo", [P, B, P], F32R, r_k + 4096)
        rden = at("rden", [P, D], F32, r_pt + 8192)
        numr = at("numr", [P, D], F32, r_pt + 6144)
        tab_raw = at("tab_raw", [P, C, 2, P], F32, r_wo)
        tab_hi = at("tab_hi", [P, C, 2, P], F32R, r_wo + 4096)
        tab_lo = at("tab_lo", [P, C, 2, P], F32R, r_wo + 8192)
        pos_i = at("pos_i", [P, T], I32, r_wo + 12288)
        pos_f = at("pos_f", [P, T], F32, r_v)
        pos_n = at("pos_n", [P, T], F32, r_v + 4096)
        onehot = at("onehot", [P, T], F32R, r_v + 8192)
        four = at("four", [P, C, D], F32, r_q)
        cf_in = at("cf_in", [P, C, 3, 40], F32, r_q + 8192)
        cm_in = at("cm_in", [P, C, 3, 40], I32, r_q + 14336 + 1024)
        cm_f = at("cm_f", [P, C, 3, 40], F32, r_q + 10624)
        ws = at("ws", [P, C, 40], F32, r_q + 12544)
        enc = at("enc", [40, D], F32, r_q + 13312)
        gk = at("gk", [40, D], F32, r_q + 18432)

        ps = ctx.enter_context(nc.psum_tensor("ps", [P, 8, 512], F32))
        S_BANK, T_BANK, O_BANK, Y_BANK = 2, 4, 6, 7

        for L in Lq:
            L.s_proj = sem(f"{L.name}_proj")
            L.s_rope = sem(f"{L.name}_rope")
            L.s_rsum = sem(f"{L.name}_rsum")
            L.s_qk_head = sem(f"{L.name}_qk_head")
            L.s_qk = sem(f"{L.name}_qk")
            L.s_v_head = sem(f"{L.name}_v_head")
            L.s_v = sem(f"{L.name}_v")
            L.s_s = sem(f"{L.name}_s")
            L.s_seen = sem(f"{L.name}_seen")
            L.s_smask = sem(f"{L.name}_smask")
            L.s_smax = sem(f"{L.name}_smax")
            L.s_nb = sem(f"{L.name}_nb")
            L.s_e = sem(f"{L.name}_e")
            L.s_rs = sem(f"{L.name}_rs")
            L.s_p = sem(f"{L.name}_p")
            L.s_t = sem(f"{L.name}_t")
            L.s_pt_head = sem(f"{L.name}_pt_head")
            L.s_pt = sem(f"{L.name}_pt")
            L.s_o = sem(f"{L.name}_o")
            L.s_o_head = sem(f"{L.name}_o_head")
            L.s_ot = sem(f"{L.name}_ot")
            L.s_y = sem(f"{L.name}_y")
            L.s_x = sem(f"{L.name}_x")
        raw_in = [sem(f"raw_in{i}") for i in range(RAW)]
        w_head = sem("w_head")
        w_done = sem("w_done")
        x_in = [sem(f"x_in{b}") for b in range(B)]
        ct_in, ct_head, ct_done = sem("ct_in"), sem("ct_head"), sem("ct_done")
        cst_in, cst = sem("cst_in"), sem("cst")
        g_in, g_tanh = sem("g_in"), sem("g_tanh")
        ln_var, ln_rstd, ln_xn = sem("ln_var"), sem("ln_rstd"), sem("ln_xn")
        ln_t, ln_head, ln_done = sem("ln_t"), sem("ln_head"), sem("ln_done")
        chain = sem("chain")
        pchain = sem("pchain")
        f_h, f_base, f_t, f_y = sem("f_h"), sem("f_base"), sem("f_t"), sem("f_y")
        f_nmax, f_exp, f_hw = sem("f_nmax"), sem("f_exp"), sem("f_hw")
        f_thead, f_tdone, f_x = sem("f_thead"), sem("f_tdone"), sem("f_x")
        b_in, b_tg, b_x = sem("b_in"), sem("b_tg"), sem("b_x")
        cn_in, k_nmax, k_exp, k_t, k_head, k_done = (sem("cn_in"), sem("k_nmax"), sem("k_exp"), sem("k_t"),
                                                     sem("k_head"), sem("k_done"))
        k_kv, k_kvs, k_kvhead, k_kvdone = sem("k_kv"), sem("k_kvs"), sem("k_kvhead"), sem("k_kvdone")
        a_exp, a_head, a_done, a_mm, a_x = sem("a_exp"), sem("a_head"), sem("a_done"), sem("a_mm"), sem("a_x")
        tab_in, tab_head, tab_done, pos_in = sem("tab_in"), sem("tab_head"), sem("tab_done"), sem("pos_in")
        oh, oh_mm, rot_out = sem("oh"), sem("oh_mm"), sem("rot_out")
        four_in, ws_done, gk_mm, gk_done, we_mm, we_done = (sem("four_in"), sem("ws_done"), sem("gk_mm"),
                                                            sem("gk_done"), sem("we_mm"), sem("we_done"))
        m_in, m_done, rot3_in = sem("m_in"), sem("m_done"), sem("rot3_in")
        out_done = sem("out_done")

        order = []
        n = 0
        for phase, tiles in (("A0", Lq[0].weight_tiles), ("F0", 6), ("F1", C), ("A2", Lq[1].weight_tiles),
                             ("F2", 6), ("A3", Lq[2].weight_tiles), ("F3", 6)):
            order.append((phase, n, tiles))
            n += tiles
        W_BASE = {phase: first for phase, first, _ in order}
        LN = {"A0": 0, "F0": 8, "A1": 16, "F1": 24, "A2": 32, "F2": 40, "A3": 48, "F3": 56}
        LNT = {"A0": 0, "F0": 8, "F1": 16, "A2": 24, "F2": 32, "A3": 40, "F3": 48}
        FN = {0: 0, 1: 8, 2: 16, 3: 24}
        FM = {0: 0, 2: 8, 3: 16}
        FB = {1: 0, 2: 1, 3: 2}

        def slot(base, n_static, n):
            s = (base + n_static) % RAW
            return s, n

        def raw_ready(engine, base, n_static, per_loop, i):
            k = base + n_static
            engine.wait_ge(raw_in[k % RAW], 16 * (k // RAW + 1) + 16 * (per_loop // RAW) * i)
            return k % RAW

        def triple(pe, dst, l_hi, l_lo, r_hi, r_lo, start, stop):
            pe.matmul(dst, l_hi, r_hi, start=start, stop=False)
            pe.matmul(dst, l_hi, r_lo, start=False, stop=False)
            return pe.matmul(dst, l_lo, r_hi, start=False, stop=stop)

        block = ctx.enter_context(nc.Block())

        @block.sync
        def _(sp):
            def load_tile(base, n_static, per_loop, i, src, cols, parts=P):
                k = base + n_static
                if k >= RAW:
                    sp.wait_ge(w_done, k - RAW + 1 + per_loop * i)
                sp.dma_start(raw[0:parts, k % RAW, 0:cols], src).then_inc(raw_in[k % RAW], 16)

            def attention(L):
                base, wp, wo = W_BASE["A" + L.name[1]], inp[L.name + "_proj"], inp[L.name + "_out"]
                for t in range(6):
                    load_tile(base, t, 0, 0, wp[0, t], C * L.hd)

                def group(i, last):
                    for h in range(GH):
                        load_tile(base, 6 + h, 10, i, wo[bass.ts(i, 1), h][0] if not isinstance(i, int) else wo[i, h],
                                  D, L.hd)
                    if not last:
                        for t in range(6):
                            load_tile(base, 10 + t, 10, i,
                                      wp[bass.ts(i + 1, 1), t][0] if not isinstance(i, int) else wp[i + 1, t],
                                      C * L.hd)
                with sp.Fori(0, L.groups - 1) as i:
                    group(i, False)
                group(L.groups - 1, True)

            def feed_forward(f):
                base = W_BASE[f"F{f}"]
                if f >= 1:
                    if f >= 2:
                        sp.wait_ge(b_x, B * (f - 1))
                    sp.dma_start(bias[:], inp[f"F{f}_bias"].broadcast_to([P, D])).then_inc(b_in, 16)
                for c in range(C):
                    load_tile(base, c, 0, 0, inp[f"F{f}_w"][c], D)
                if f != 1:
                    load_tile(base, C, 0, 0, inp[f"F{f}_ag"], C * FF[f]["cols"])
                    load_tile(base, C + 1, 0, 0, inp[f"F{f}_b"], D, FF[f]["er"])

            sp.dma_start(consts[:], inp["consts"]).then_inc(cst_in, 16)
            for b in range(B):
                sp.dma_start(x[:, b, :], inp["x"][b]).then_inc(x_in[b], 16)
            sp.dma_start(gates[:], inp["gates"].broadcast_to([P, 8])).then_inc(g_in, 16)
            sp.dma_start(bthr[:], inp["b_thr"].broadcast_to([P, 1])).then_inc(g_in, 16)
            for c in range(C):
                sp.dma_start(ct_raw[:, c, :], inp["ctx_t"][c]).then_inc(ct_in, 16)
            attention(Lq[0])
            feed_forward(0)
            sp.wait_ge(Lq[0].s_s, B * Lq[0].groups)
            sp.dma_start(cn_raw[:], inp["ctx"]).then_inc(cn_in, 16)
            sp.wait_ge(Lq[0].s_y, B * Lq[0].groups)
            sp.dma_start(tab_raw[:], inp["rope2"]).then_inc(tab_in, 16)
            sp.dma_start(pos_i[:], inp["pos"].broadcast_to([P, T])).then_inc(pos_in, 16)
            sp.wait_ge(f_x, B)
            sp.wait_ge(k_exp, B)
            sp.dma_start(four[:], inp["fourier"]).then_inc(four_in, 16)
            sp.dma_start(cf_in[:], inp["F1_coef"]).then_inc(four_in, 16)
            sp.dma_start(cm_in[:], inp["F1_mask"]).then_inc(four_in, 16)
            sp.dma_start(enc[:], inp["F1_enc"]).then_inc(four_in, 16)
            feed_forward(1)
            sp.wait_ge(oh_mm, C)
            sp.dma_start(mask_in[:], inp["mask"]).then_inc(m_in, 16)
            sp.dma_start(causal[:], inp["causal"]).then_inc(m_in, 16)
            attention(Lq[1])
            feed_forward(2)
            sp.wait_ge(Lq[1].s_rope, Lq[1].ready("KQ", Lq[1].groups - 1, 1))
            sp.dma_start(rot3[:], inp["rope3"]).then_inc(rot3_in, 16)
            attention(Lq[2])
            feed_forward(3)
            for b in range(B):
                sp.wait_ge(f_x, FN[3] + b + 1)
                sp.dma_start(out[b], x[:, b, :]).then_inc(out_done, 16)
            sp.wait_ge(out_done, 16 * B)

        @block.tensor
        def _(pe):
            def norm_transpose(phase, b):
                n = LNT[phase] + b
                pe.wait_ge(ln_xn, LN[phase] + b + 1)
                if n >= 2:
                    pe.wait_ge(ln_done, n - 1)
                for c in range(C):
                    mm = pe.transpose(ps[:, b % 2, c * P:(c + 1) * P], xn[:, b % 2, c * P:(c + 1) * P], ident)
                mm.then_inc(ln_t, 1)

            def attention(L, phase):
                base, hd = W_BASE[phase], L.hd

                def fillers(b, i, when=NOW):
                    half = L.half[b]
                    tok = slice(half * HALF * P, (half + 1) * HALF * P)
                    ahead = 0 if when == PROLOGUE or b < 3 else 1
                    for k, (kind, n) in enumerate(L.fill[b]):
                        t, bank = L.tile(i, b, k, when)
                        last_user = L.two_before(b, k, when)
                        if last_user:
                            pb, pk, pw = last_user
                            if L.fill[pb][pk][0] == "V":
                                pe.wait_ge(L.s_v, L.index("V", i, pb, pk, pw) + 1)
                            elif L.rope:
                                pe.wait_ge(L.s_rope, L.index("KQ", i, pb, pk, pw) + 1)
                            else:
                                pe.wait_ge(L.s_qk, L.index("KQ", i, pb, pk, pw) + 1)
                        w = WEIGHT_ORDER[(kind, n) if kind == "Q" else kind]
                        if when == PROLOGUE:
                            pe.wait_ge(w_done, base + w + 1)
                        else:
                            pe.wait_ge(w_done, (i + ahead) * 10 + (base + w + 1))
                        src_hi, src_lo = (xt_hi, xt_lo) if kind == "Q" or n == 1 else (ct_hi, ct_lo)
                        if kind == "V":
                            for j in range(HALF):
                                rows = slice((half * HALF + j) * P, (half * HALF + j + 1) * P)
                                for c in range(C):
                                    mm = triple(pe, ps[:, bank, j * hd:(j + 1) * hd], src_hi[:, c, rows],
                                                src_lo[:, c, rows], L.wkv_hi[:, 1, c, :], L.wkv_lo[:, 1, c, :],
                                                c == 0, c == C - 1)
                        else:
                            w_hi, w_lo = ((L.wq_hi[:, n], L.wq_lo[:, n]) if kind == "Q"
                                          else (L.wkv_hi[:, 0], L.wkv_lo[:, 0]))
                            for c in range(C):
                                mm = triple(pe, ps[0:hd, bank, :], w_hi[:, c, :], w_lo[:, c, :],
                                            src_hi[:, c, tok], src_lo[:, c, tok], c == 0, c == C - 1)
                        mm.then_inc(L.s_proj, 1)

                def scores(b, i):
                    bank = S_BANK + (b % 2 if L.sources == 1 else 0)
                    pe.wait_ge(L.s_e, B * i + b + 1)
                    if b % HALF == 0:
                        pe.wait_ge(L.s_qk, L.ready("KQ", i, b // HALF))
                    for h in range(GH):
                        at_ = ps[:, bank + h * L.keys // 512, (h * L.keys) % 512:(h * L.keys) % 512 + L.keys]
                        mm = triple(pe, at_, L.q_hi[0:hd, h, b * P:(b + 1) * P], L.q_lo[0:hd, h, b * P:(b + 1) * P],
                                    L.k_hi[0:hd, b].rearrange("p s k -> p (s k)"),
                                    L.k_lo[0:hd, b].rearrange("p s k -> p (s k)"), True, True)
                    mm.then_inc(L.s_s, 1)

                def transposes(b, i):
                    pe.wait_ge(L.s_p, B * i + b + 1)
                    for h in range(GH):
                        for s in range(L.sources):
                            at_ = (h * L.sources + s) * P
                            mm = pe.transpose(ps[:, T_BANK + s, h * P:(h + 1) * P], probs[:, at_:at_ + P], ident)
                    mm.then_inc(L.s_t, 1)

                def heads_out(b, i):
                    pe.wait_ge(L.s_pt, B * i + b + 1)
                    if b % HALF == 0:
                        pe.wait_ge(L.s_v, L.ready("V", i, b // HALF))
                    for s in range(L.sources):
                        mm = triple(pe, ps[0:hd, O_BANK, :], L.v_hi[:, b, s], L.v_lo[:, b, s],
                                    L.pt_hi[:, s], L.pt_lo[:, s], s == 0, s == L.sources - 1)
                    mm.then_inc(L.s_o, 1)

                def out_proj(b, i):
                    pe.wait_ge(L.s_ot, B * i + b + 1)
                    pe.wait_ge(L.s_x, B * i + b + 1)
                    if b == 0:
                        pe.wait_ge(w_done, base + 10 + 10 * i)
                    for h in range(GH):
                        mm = triple(pe, ps[:, Y_BANK, :], ot_hi[0:hd, h * P:(h + 1) * P],
                                    ot_lo[0:hd, h * P:(h + 1) * P], L.wo_hi[0:hd, h], L.wo_lo[0:hd, h],
                                    h == 0, h == GH - 1)
                    mm.then_inc(L.s_y, 1)

                def group(i, last):
                    for b in range(B):
                        scores(b, i)
                        if b >= 1:
                            transposes(b - 1, i)
                        if b >= 2:
                            out_proj(b - 2, i)
                        if b >= 1:
                            heads_out(b - 1, i)
                        if not last or b < 3:
                            fillers(b, i)
                    transposes(B - 1, i)
                    out_proj(B - 2, i)
                    heads_out(B - 1, i)
                    out_proj(B - 1, i)

                for b in range(3, 8):
                    fillers(b, 0, PROLOGUE)
                with pe.Fori(0, L.groups - 1) as i:
                    group(i, False)
                group(L.groups - 1, True)

            def feed_forward(f):
                F, base = FF[f], W_BASE[f"F{f}"]
                er, phase = F["er"], f"F{f}"

                def products(b):
                    rows = slice(b * P, (b + 1) * P)
                    pe.wait_ge(ln_done, LNT[phase] + b + 1)
                    if b == 0:
                        pe.wait_ge(w_done, base + (C + 2 if er else C))
                    if er:
                        if b >= 2:
                            pe.wait_ge(f_tdone, FM[f] + b - 1)
                        for c in range(C):
                            mm = triple(pe, ps[:, 2 + b % 2, 0:F["cols"]], xt_hi[:, c, rows], xt_lo[:, c, rows],
                                        F["ag_hi"][:, c], F["ag_lo"][:, c], c == 0, c == C - 1)
                        mm.then_inc(f_h, 1)
                    if b >= 4:
                        pe.wait_ge(f_x, FN[f] + b - 3)
                    for c in range(C):
                        mm = triple(pe, ps[:, 4 + b % 4, :], xt_hi[:, c, rows], xt_lo[:, c, rows],
                                    wt_hi[:, c], wt_lo[:, c], c == 0, c == C - 1 and not er)
                    if not er:
                        mm.then_inc(f_y, 1)

                def experts(b):
                    pe.wait_ge(f_hw, FM[f] + b + 1)
                    pe.transpose(ps[0:er, 2 + b % 2, 256:384], hw[:, b % 2, 0:er], ident).then_inc(f_t, 1)
                    pe.wait_ge(f_tdone, FM[f] + b + 1)
                    triple(pe, ps[:, 4 + b % 4, :], hwt_hi[0:er], hwt_lo[0:er], F["lb_hi"][0:er], F["lb_lo"][0:er],
                           False, True).then_inc(f_y, 1)

                for s in range(B + 4):
                    if 1 <= s <= B:
                        norm_transpose(phase, s - 1)
                    if er and s >= 4:
                        experts(s - 4)
                    if 2 <= s <= B + 1:
                        products(s - 2)

            def l1_keys():
                for b in range(B):
                    pe.wait_ge(k_exp, b + 1)
                    for c in range(C):
                        mm = pe.transpose(ps[:, 0, c * P:(c + 1) * P], probs[:, c * P:(c + 1) * P], ident)
                    mm.then_inc(k_t, 1)
                    pe.wait_ge(k_done, b + 1)
                    for c in range(C):
                        mm = triple(pe, ps[:, 1, 0:P], kt_hi[:, c], kt_lo[:, c], ct_hi[:, c, b * P:(b + 1) * P],
                                    ct_lo[:, c, b * P:(b + 1) * P], c == 0, c == C - 1)
                    mm.then_inc(k_kv, 1)

            def l1_attention():
                for b in range(B):
                    pe.wait_ge(a_done, b + 1)
                    if b == 0:
                        pe.wait_ge(k_kvdone, B)
                    if b >= 2:
                        pe.wait_ge(a_x, b - 1)
                    den, num = 2 + 2 * (b % 2), 3 + 2 * (b % 2)
                    pe.matmul(ps[:, den, :], blk_r[:], ot_hi[:], start=True, stop=False)
                    pe.matmul(ps[:, den, :], blk_r[:], ot_lo[:], start=False, stop=True)
                    triple(pe, ps[:, num, :], kvs_hi[:, b], kvs_lo[:, b], ot_hi[:], ot_lo[:],
                           True, True).then_inc(a_mm, 1)

            def rope_tables():
                pe.wait_ge(tab_done, 1)
                for c in range(C):
                    pe.wait_ge(oh, c + 1)
                    for t in range(2):
                        for half in range(2):
                            bank, tok = 2 * t + half, slice(half * 512, (half + 1) * 512)
                            pe.matmul(ps[:, bank, :], tab_hi[:, c, t], onehot[:, tok], start=c == 0, stop=False)
                            mm = pe.matmul(ps[:, bank, :], tab_lo[:, c, t], onehot[:, tok], start=False,
                                           stop=c == C - 1)
                    mm.then_inc(oh_mm, 1)

            def l1_weight():
                pe.wait_ge(four_in, 64)
                pe.wait_ge(ws_done, 1)
                for c in range(C):
                    mm = pe.matmul(ps[0:40, 0, :], ws[:, c], four[:, c], start=c == 0, stop=c == C - 1)
                mm.then_inc(gk_mm, 1)
                pe.wait_ge(gk_done, 1)
                for c in range(C):
                    pe.matmul(ps[:, 4 + c, :], enc[:, c * P:(c + 1) * P], gk[:], start=True,
                              stop=True).then_inc(we_mm, 1)

            pe.wait_ge(cst, 1)
            for b in range(B):
                norm_transpose("A0", b)
            pe.wait_ge(ct_done, C)
            pe.wait_ge(ln_done, B)
            attention(Lq[0], "A0")
            feed_forward(0)
            pe.wait_ge(f_x, B)
            l1_keys()
            pe.wait_ge(k_kvs, B)
            rope_tables()
            pe.wait_ge(rot_out, 1)
            l1_attention()
            pe.wait_ge(a_x, B)
            l1_weight()
            pe.wait_ge(we_done, C)
            feed_forward(1)
            pe.wait_ge(f_x, 2 * B)
            for b in range(B):
                norm_transpose("A2", b)
            pe.wait_ge(ln_done, LNT["A2"] + B)
            attention(Lq[1], "A2")
            feed_forward(2)
            pe.wait_ge(f_x, 3 * B)
            for b in range(B):
                norm_transpose("A3", b)
            pe.wait_ge(ln_done, LNT["A3"] + B)
            attention(Lq[2], "A3")
            feed_forward(3)

        @block.vector
        def _(v):
            links = [0]

            def link(ins):
                links[0] += 1
                ins.then_inc(chain, 1)
                v.wait_ge(chain, links[0])

            def norm_stats(phase, b, n):
                n = LN[phase] + b
                link(v.bn_stats(stats[:, b % 2], x[:, b]))
                link(v.bn_aggr(mv[:, b % 2], stats[:, b % 2]))
                if n >= 2:
                    v.wait_ge(ln_rstd, n - 1)
                v.tensor_scalar(ve[:, b % 2:b % 2 + 1], mv[:, b % 2, 1:2], LN_EPS, None, ALU.add).then_inc(ln_var, 1)

            def norm_rows(phase, b):
                n = LN[phase] + b
                v.wait_ge(ln_rstd, n + 1)
                if phase != "A1" and b >= 2:
                    v.wait_ge(ln_t, LNT[phase] + b - 1)
                if phase == "A1" and b >= 2:
                    v.wait_ge(a_exp, b - 1)
                v.tensor_scalar(xn[:, b % 2], x[:, b], mv[:, b % 2, 0:1], rstd[:, b % 2:b % 2 + 1],
                                ALU.subtract, ALU.mult).then_inc(ln_xn, 1)

            def norm_tail(phase, b):
                n = LNT[phase] + b
                v.wait_ge(ln_head, n + 1)
                cols = slice(b * P, (b + 1) * P)
                v.tensor_tensor(xt_lo[:, :, cols], ps[:, b % 2, :].rearrange("p (c t) -> p c t", c=C),
                                xt_hi[:, :, cols], ALU.subtract).then_inc(ln_done, 1)

            def norm_all(phase):
                for s in range(B + 2):
                    if s < B:
                        norm_stats(phase, s, s)
                    if 1 <= s <= B:
                        norm_rows(phase, s - 1)
                    if s >= 2:
                        norm_tail(phase, s - 2)

            def attention(L, phase):
                hd = L.hd

                def evacuate(b, k, i, when=NOW):
                    kind, n = L.fill[b][k]
                    half = L.half[b]
                    batches = slice(half * HALF, (half + 1) * HALF)
                    t, bank = L.tile(i, b, k, when)
                    if kind == "V":
                        v.wait_ge(L.s_v_head, L.index("V", i, b, k, when) + 1)
                        v.tensor_tensor(L.v_lo[:, batches, n],
                                        ps[:, bank, 0:HALF * hd].rearrange("p (b d) -> p b d", b=HALF),
                                        L.v_hi[:, batches, n], ALU.subtract).then_inc(L.s_v, 1)
                        return
                    m = L.index("KQ", i, b, k, when)
                    if not L.rope:
                        v.wait_ge(L.s_qk_head, m + 1)
                        if kind == "K":
                            hi, lo = (w[0:hd, batches, n] for w in (L.k_hi, L.k_lo))
                        else:
                            hi, lo = (w[0:hd, n, half * HALF * P:(half + 1) * HALF * P]
                                      .rearrange("p (b t) -> p b t", b=HALF) for w in (L.q_hi, L.q_lo))
                        v.tensor_tensor(lo, ps[0:hd, bank, :].rearrange("p (b t) -> p b t", b=HALF), hi,
                                        ALU.subtract).then_inc(L.s_qk, 1)
                        return
                    v.wait_ge(L.s_proj, t + 1)
                    if when != PROLOGUE or m >= 1:
                        v.wait_ge(L.s_rsum, m)
                    if when != PROLOGUE or m >= 2:
                        v.wait_ge(L.s_qk, m - 1)
                    a = L.index("KQ", 0, b, k, when) % 2
                    hp = P // 2
                    view = lambda ap: ap.rearrange("p (b t) -> p b t", b=HALF)
                    if L.name == "L2":
                        tok = slice(half * 512, (half + 1) * 512)
                        cos, sin = view(cos2[:, tok]), view(sin2[:, tok])
                    else:
                        cos, sin = (rot3[:, j:j + 1, :].to_broadcast([P, HALF, P]) for j in range(2))
                    v.tensor_tensor(view(rope_a[:, a]), view(ps[:, bank, :]), cos, ALU.mult)
                    v.tensor_tensor(view(rope_b[0:hp]), view(ps[hp:P, bank, :]), sin[0:hp], ALU.mult)
                    v.tensor_tensor(view(rope_b[hp:P]), view(ps[0:hp, bank, :]), sin[hp:P],
                                    ALU.mult).then_inc(L.s_rope, 1)

                def row_max(b, i):
                    bank = S_BANK + (b % 2 if L.sources == 1 else 0)
                    v.wait_ge(L.s_s, B * i + b + 1)
                    if L.rope:
                        v.sem_inc(L.s_seen, 1)
                    sc = ps[:, bank:bank + L.sources, :].rearrange("p n (g k) -> p (n g) k", k=L.keys)
                    if L.rope:
                        which = 0 if L.name == "L2" else 1
                        m = mask2[:, b:b + 1, :] if L.name == "L2" else mask3[:, 0:1, :]
                        v.copy_predicated(sc, m.to_broadcast([P, GH, P]),
                                          fill[:, which:which + 1].unsqueeze(2).to_broadcast([P, GH, P])
                                          ).then_inc(L.s_smask, 1)
                        v.wait_ge(L.s_smask, B * i + b + 1)
                    v.tensor_reduce(negmax[:, b % 2], sc, X_AXIS, ALU.max, negate=True).then_inc(L.s_smax, 1)
                    v.wait_ge(L.s_smax, B * i + b + 1)
                    v.tensor_scalar(nbias[:, b % 2], negmax[:, b % 2], L.scale, None, ALU.mult).then_inc(L.s_nb, 1)

                def row_sum(b, i):
                    v.wait_ge(L.s_e, B * i + b + 1 + (2 // L.sources))
                    v.reciprocal(rsums[:, b % 2], sums[:, b % 2]).then_inc(L.s_rs, 1)

                def pt_tail(b, i):
                    v.wait_ge(L.s_pt_head, B * i + b + 1)
                    v.tensor_tensor(L.pt_lo[:], ps[:, T_BANK:T_BANK + L.sources, :], L.pt_hi[:],
                                    ALU.subtract).then_inc(L.s_pt, 1)

                def ot_tail(b, i):
                    v.wait_ge(L.s_o_head, B * i + b + 1)
                    v.tensor_tensor(ot_lo[0:hd], ps[0:hd, O_BANK, :], ot_hi[0:hd], ALU.subtract).then_inc(L.s_ot, 1)

                def residual(b, i):
                    v.wait_ge(L.s_y, B * i + b + 1)
                    v.scalar_tensor_tensor(out=x[:, b], in0=ps[:, Y_BANK, :], scalar=tg[:, L.gate:L.gate + 1],
                                           in1=x[:, b], op0=ALU.mult, op1=ALU.add).then_inc(L.s_x, 1)

                def group(i, last):
                    for b in range(B):
                        row_max(b, i)
                        if b >= 1:
                            pt_tail(b - 1, i)
                        if b == 0:
                            evacuate(7, len(L.fill[7]) - 1, i, BEFORE)
                        elif not last or b <= 3:
                            evacuate(b - 1, len(L.fill[b - 1]) - 1, i)
                        if b >= 2:
                            residual(b - 2, i)
                        row_sum(b, i)
                        if b >= 1:
                            ot_tail(b - 1, i)
                        if (not last or b < 3) and len(L.fill[b]) == 2:
                            evacuate(b, 0, i)
                    pt_tail(B - 1, i)
                    residual(B - 2, i)
                    ot_tail(B - 1, i)
                    residual(B - 1, i)

                v.sem_inc(L.s_x, 1)
                for b in range(3, 8):
                    for k in range(len(L.fill[b])):
                        if (b, k) != (7, len(L.fill[7]) - 1):
                            evacuate(b, k, 0, PROLOGUE)
                with v.Fori(0, L.groups - 1) as i:
                    group(i, False)
                group(L.groups - 1, True)
                v.wait_ge(L.s_x, B * L.groups + 1)

            def top2_gate(f, b):
                er, bank = FF[f]["er"], 2 + b % 2
                m = FM[f] + b
                logits = ps[:, bank, er:er + NE]
                bc = lambda col: col.to_broadcast([P, NE])
                e = gt[:, 0]
                v.wait_ge(f_h, m + 1)
                v.tensor_reduce(thr[:, 0:1], logits, X_AXIS, ALU.max, negate=True).then_inc(f_nmax, 1)
                v.wait_ge(f_exp, m + 1)
                link(v.tensor_reduce(gt[:, 1, 0:1], e, X_AXIS, ALU.max))
                link(v.scalar_tensor_tensor(out=gt[:, 2], in0=e, scalar=gt[:, 1, 0:1], in1=iota8,
                                            op0=ALU.is_ge, op1=ALU.mult))
                link(v.tensor_reduce(gt[:, 3, 0:1], gt[:, 2], X_AXIS, ALU.max))
                link(v.tensor_scalar(gt[:, 4], gt[:, 2], gt[:, 3, 0:1], None, ALU.is_equal))
                link(v.scalar_tensor_tensor(out=gt[:, 5], in0=gt[:, 4], scalar=-2.0, in1=e,
                                            op0=ALU.mult, op1=ALU.add))
                link(v.tensor_reduce(gt[:, 6, 0:1], gt[:, 5], X_AXIS, ALU.max))
                link(v.scalar_tensor_tensor(out=gt[:, 7], in0=gt[:, 5], scalar=gt[:, 6, 0:1], in1=iota8,
                                            op0=ALU.is_ge, op1=ALU.mult))
                link(v.tensor_reduce(gt[:, 8, 0:1], gt[:, 7], X_AXIS, ALU.max))
                link(v.scalar_tensor_tensor(out=gt[:, 9], in0=gt[:, 7], scalar=gt[:, 8, 0:1], in1=gt[:, 4],
                                            op0=ALU.is_equal, op1=ALU.add))
                link(v.tensor_tensor(gt[:, 10], gt[:, 9], e, ALU.mult))
                link(v.tensor_reduce(gt[:, 11, 0:1], gt[:, 10], X_AXIS, ALU.add))
                link(v.reciprocal(gt[:, 12, 0:1], gt[:, 11, 0:1]))
                link(v.tensor_scalar(gt[:, 13], gt[:, 10], gt[:, 12, 0:1], 2.0, ALU.mult, ALU.mult))
                weigh(f, b)

            def threshold_gate(f, b):
                er, bank = FF[f]["er"], 2 + b % 2
                m = FM[f] + b
                v.wait_ge(f_h, m + 1)
                v.tensor_reduce(thr[:, 0:1], ps[:, bank, er:er + NE], X_AXIS, ALU.max, negate=True).then_inc(f_nmax, 1)
                v.wait_ge(f_exp, m + 1)
                v.reciprocal(gt[:, 1, 0:1], thr[:, 1:2])
                link(v.tensor_scalar(gt[:, 2, 0:1], thr[:, 2:3], 1.0, None, ALU.add))
                link(v.reciprocal(gt[:, 3, 0:1], gt[:, 2, 0:1]))
                link(v.tensor_scalar(gt[:, 4, 0:1], gt[:, 3, 0:1], 0.125, None, ALU.mult))
                link(v.tensor_scalar(gt[:, 5], gt[:, 0], gt[:, 1, 0:1], gt[:, 4, 0:1], ALU.mult, ALU.subtract))
                link(v.tensor_scalar(gt[:, 6], gt[:, 5], 0.0, None, ALU.max))
                link(v.tensor_reduce(gt[:, 7, 0:1], gt[:, 6], X_AXIS, ALU.add))
                link(v.scalar_tensor_tensor(out=gt[:, 8, 0:1], in0=gt[:, 7, 0:1], scalar=0.0, in1=gt[:, 7, 0:1],
                                            op0=ALU.is_equal, op1=ALU.add))
                link(v.reciprocal(gt[:, 9, 0:1], gt[:, 8, 0:1]))
                link(v.tensor_scalar(gt[:, 13], gt[:, 6], gt[:, 9, 0:1], 2.0, ALU.mult, ALU.mult))
                weigh(f, b)

            def weigh(f, b):
                er, bank, m = FF[f]["er"], 2 + b % 2, FM[f] + b
                if m >= 2:
                    v.wait_ge(f_t, m - 1)
                v.tensor_tensor(hw[:, b % 2, 0:er].rearrange("p (e r) -> p e r", e=NE),
                                ps[:, bank, 0:er].rearrange("p (e r) -> p e r", e=NE),
                                gt[:, 13].unsqueeze(2).to_broadcast([P, NE, er // NE]), ALU.mult).then_inc(f_hw, 1)

            def feed_forward(f):
                F, phase, gate = FF[f], f"F{f}", 2 * f + 1
                er = F["er"]
                if f >= 1:
                    v.wait_ge(b_in, 16 * (FB[f] + 1))
                    v.tensor_scalar(bias[:], bias[:], tg[:, gate:gate + 1], None, ALU.mult).then_inc(b_tg, 1)
                for s in range(B + 5):
                    if s < B:
                        norm_stats(phase, s, s)
                    if 1 <= s <= B:
                        norm_rows(phase, s - 1)
                    if 2 <= s <= B + 1:
                        norm_tail(phase, s - 2)
                    if er and 3 <= s <= B + 2:
                        (threshold_gate if f == 3 else top2_gate)(f, s - 3)
                    if er and 4 <= s <= B + 3:
                        b = s - 4
                        v.wait_ge(f_thead, FM[f] + b + 1)
                        v.tensor_tensor(hwt_lo[0:er], ps[0:er, 2 + b % 2, 256:384], hwt_hi[0:er],
                                        ALU.subtract).then_inc(f_tdone, 1)
                    if 5 <= s:
                        b = s - 5
                        v.wait_ge(f_y, FN[f] + b + 1)
                        if f >= 1:
                            v.wait_ge(b_x, FB[f] * B + b + 1)
                        v.scalar_tensor_tensor(out=x[:, b], in0=ps[:, 4 + b % 4, :], scalar=tg[:, gate:gate + 1],
                                               in1=x[:, b], op0=ALU.mult, op1=ALU.add).then_inc(f_x, 1)
                v.wait_ge(f_x, FN[f] + B)

            def l1_keys():
                v.wait_ge(cn_in, 16)
                for b in range(B):
                    v.tensor_reduce(negmax[:, b % 2, 0:1], cn_raw[:, b], X_AXIS, ALU.max,
                                    negate=True).then_inc(k_nmax, 1)
                    v.wait_ge(k_head, b + 1)
                    v.tensor_tensor(kt_lo[:], ps[:, 0, :].rearrange("p (c k) -> p c k", c=C), kt_hi[:],
                                    ALU.subtract).then_inc(k_done, 1)
                    link(v.reciprocal(rsums[:, b % 2, 0:1], sums[:, b % 2, 0:1]))
                    v.wait_ge(k_kv, b + 1)
                    v.scalar_tensor_tensor(out=kvs[:], in0=ps[:, 1, 0:P], scalar=rsums[:, b % 2, 0:1], in1=blk,
                                           op0=ALU.mult, op1=ALU.mult).then_inc(k_kvs, 1)
                    v.wait_ge(k_kvhead, b + 1)
                    v.tensor_tensor(kvs_lo[:, b], kvs[:], kvs_hi[:, b], ALU.subtract).then_inc(k_kvdone, 1)

            def rope_tables():
                v.wait_ge(tab_head, 1)
                v.tensor_tensor(tab_lo[:], tab_raw[:], tab_hi[:], ALU.subtract).then_inc(tab_done, 1)
                v.wait_ge(pos_in, 16)
                link(v.tensor_copy(pos_f[:], pos_i[:]))
                link(v.tensor_scalar(pos_n[:], pos_f[:], 0.0, float(C * P), ALU.is_lt, ALU.mult))
                link(v.tensor_tensor(pos_f[:], pos_f[:], pos_n[:], ALU.add))
                link(v.tensor_scalar(pos_f[:], pos_f[:], 0.0, float(C * P - 1), ALU.max, ALU.min))
                for c in range(C):
                    if c >= 1:
                        v.wait_ge(oh_mm, c)
                    v.tensor_scalar(onehot[:], pos_f[:], pidx[:, c:c + 1], None, ALU.is_equal).then_inc(oh, 1)
                v.wait_ge(oh_mm, C)
                v.tensor_copy(cos2[:], ps[:, 0:2, :].rearrange("p a b -> p (a b)"))
                v.tensor_copy(sin2[:], ps[:, 2:4, :].rearrange("p a b -> p (a b)")).then_inc(rot_out, 1)
                v.wait_ge(rot_out, 1)

            def l1_attention():
                for s in range(B + 3):
                    if s < B:
                        norm_stats("A1", s, s)
                    if 1 <= s <= B:
                        norm_rows("A1", s - 1)
                    if 2 <= s <= B + 1:
                        b = s - 2
                        v.wait_ge(a_head, b + 1)
                        v.tensor_tensor(ot_lo[:], probs[:, 0:D], ot_hi[:], ALU.subtract).then_inc(a_done, 1)
                    if s >= 3:
                        b = s - 3
                        den, num = 2 + 2 * (b % 2), 3 + 2 * (b % 2)
                        v.wait_ge(a_mm, b + 1)
                        link(v.reciprocal(rden[:], ps[:, den, :]))
                        link(v.tensor_tensor(numr[:], ps[:, num, :], rden[:], ALU.mult))
                        v.scalar_tensor_tensor(out=x[:, b], in0=numr[:], scalar=tg[:, 2:3], in1=x[:, b],
                                               op0=ALU.mult, op1=ALU.add).then_inc(a_x, 1)
                v.wait_ge(a_x, B)

            def l1_weight():
                v.wait_ge(four_in, 64)
                link(v.tensor_copy(cm_f[:], cm_in[:]))
                link(v.tensor_tensor(cf_in[:], cf_in[:], cm_f[:], ALU.mult))
                link(v.tensor_tensor(ws[:], cf_in[:, :, 0], cf_in[:, :, 1], ALU.add))
                v.tensor_tensor(ws[:], ws[:], cf_in[:, :, 2], ALU.add).then_inc(ws_done, 1)
                v.wait_ge(gk_mm, 1)
                v.tensor_scalar(gk[:], ps[0:40, 0, :], 0.5, None, ALU.mult).then_inc(gk_done, 1)
                base = W_BASE["F1"]
                for c in range(C):
                    s = raw_ready(v, base, c, 0, 0)
                    v.wait_ge(we_mm, c + 1)
                    v.tensor_tensor(raw[:, s, 0:D], ps[:, 4 + c, :], raw[:, s, 0:D], ALU.add).then_inc(we_done, 1)

            v.memset(minus_half[:], -0.5)
            v.memset(fill[:, 0:1], -1.0e9 * float(P) ** 0.5)
            v.memset(fill[:, 1:2], -3.4028234e38).then_inc(cst, 1)
            v.wait_ge(cst_in, 16)
            v.tensor_copy(blk_r[:], blk).then_inc(cst, 1)
            for b in range(B):
                v.wait_ge(x_in[b], 16)
            norm_all("A0")
            for c in range(C):
                v.wait_ge(ct_head, c + 1)
                v.tensor_tensor(ct_lo[:, c], ct_raw[:, c], ct_hi[:, c], ALU.subtract).then_inc(ct_done, 1)
            v.wait_ge(g_tanh, 2)
            attention(Lq[0], "A0")
            feed_forward(0)
            l1_keys()
            rope_tables()
            l1_attention()
            l1_weight()
            feed_forward(1)
            norm_all("A2")
            v.wait_ge(m_in, 32)
            v.tensor_scalar(mask2[:], mask_in[:], 0.0, None, ALU.is_equal)
            v.tensor_scalar(mask3[:, 0], causal[:], 0.0, None, ALU.is_equal).then_inc(m_done, 1)
            v.wait_ge(m_done, 1)
            attention(Lq[1], "A2")
            feed_forward(2)
            norm_all("A3")
            v.wait_ge(rot3_in, 16)
            attention(Lq[2], "A3")
            feed_forward(3)

        @block.scalar
        def _(act):
            def norm_head(phase, b):
                n = LNT[phase] + b
                act.wait_ge(ln_t, n + 1)
                act.copy(xt_hi[:, :, b * P:(b + 1) * P],
                         ps[:, b % 2, :].rearrange("p (c t) -> p c t", c=C)).then_inc(ln_head, 1)

            def weight_head(base, n_static, per_loop, i, dst, cols, parts=P):
                s = raw_ready(act, base, n_static, per_loop, i)
                act.copy(dst, raw[0:parts, s, 0:cols]).then_inc(w_head, 1)

            def attention(L, phase):
                base, hd = W_BASE[phase], L.hd

                def proj_weight(t, i, n_static, per_loop):
                    dst = {0: L.wq_hi[:, 0], 1: L.wkv_hi[:, 0], 2: L.wq_hi[:, 1], 3: L.wkv_hi[:, 1],
                           4: L.wq_hi[:, 2], 5: L.wq_hi[:, 3]}[t]
                    weight_head(base, n_static, per_loop, i, dst.rearrange("p c d -> p (c d)"), C * hd)

                def head(b, k, i, when=NOW):
                    kind, n = L.fill[b][k]
                    half = L.half[b]
                    t, bank = L.tile(i, b, k, when)
                    m, a = L.index("KQ", i, b, k, when), L.index("KQ", 0, b, k, when) % 2
                    if kind == "V":
                        act.wait_ge(L.s_proj, t + 1)
                        act.copy(L.v_hi[:, half * HALF:(half + 1) * HALF, n],
                                 ps[:, bank, 0:HALF * hd].rearrange("p (b d) -> p b d", b=HALF)
                                 ).then_inc(L.s_v_head, 1)
                        return
                    if kind == "K":
                        dst = L.k_hi[0:hd, half * HALF:(half + 1) * HALF, n]
                    else:
                        dst = L.q_hi[0:hd, n, half * HALF * P:(half + 1) * HALF * P].rearrange(
                            "p (b t) -> p b t", b=HALF)
                    if L.rope:
                        act.wait_ge(L.s_rsum, m + 1)
                        src = rope_a[:, a]
                    else:
                        act.wait_ge(L.s_proj, t + 1)
                        src = ps[0:hd, bank, :]
                    act.copy(dst, src.rearrange("p (b t) -> p b t", b=HALF)).then_inc(L.s_qk_head, 1)

                def exps(b, i):
                    bank = S_BANK + (b % 2 if L.sources == 1 else 0)
                    act.wait_ge(L.s_nb, B * i + b + 1)
                    for h in range(GH):
                        at_ = h * L.keys
                        e = act.activation(probs[:, at_:at_ + L.keys],
                                           ps[:, bank + at_ // 512, at_ % 512:at_ % 512 + L.keys], ACT.Exp,
                                           bias=nbias[:, b % 2, h:h + 1], scale=L.scale,
                                           accum_out=sums[:, b % 2, h:h + 1])
                    e.then_inc(L.s_e, 1)

                def pt_head(b, i):
                    act.wait_ge(L.s_t, B * i + b + 1)
                    act.copy(L.pt_hi[:], ps[:, T_BANK:T_BANK + L.sources, :]).then_inc(L.s_pt_head, 1)

                def o_head(b, i):
                    act.wait_ge(L.s_o, B * i + b + 1)
                    act.copy(ot_hi[0:hd], ps[0:hd, O_BANK, :]).then_inc(L.s_o_head, 1)

                def group(i, last):
                    for b in range(B):
                        if b >= 1:
                            pt_head(b - 1, i)
                        late = b == 0 or not last or b <= 3
                        if late and not L.rope:
                            head((b - 1) % 8, len(L.fill[(b - 1) % 8]) - 1, i, NOW if b else BEFORE)
                        exps(b, i)
                        if late and L.rope:
                            head((b - 1) % 8, len(L.fill[(b - 1) % 8]) - 1, i, NOW if b else BEFORE)
                        if b >= 1:
                            o_head(b - 1, i)
                        if (not last or b < 3) and len(L.fill[b]) == 2:
                            head(b, 0, i)
                        if b == 0:
                            act.wait_ge(L.s_x, B * i + 1)
                            for h in range(GH):
                                weight_head(base, 6 + h, 10, i, L.wo_hi[0:hd, h], D, hd)
                        elif not last:
                            for t in SPLIT_AT.get(b, []):
                                proj_weight(t, i, 10 + t, 10)
                    pt_head(B - 1, i)
                    o_head(B - 1, i)

                act.sem_inc(L.s_e, 2 // L.sources)
                for t in range(6):
                    proj_weight(t, 0, t, 0)
                for b in range(3, 8):
                    for k in range(len(L.fill[b])):
                        if (b, k) != (7, len(L.fill[7]) - 1):
                            head(b, k, 0, PROLOGUE)
                with act.Fori(0, L.groups - 1) as i:
                    group(i, False)
                group(L.groups - 1, True)

            def ff_weights(f):
                F, base = FF[f], W_BASE[f"F{f}"]
                if f == 1:
                    act.wait_ge(we_done, C)
                for c in range(C):
                    weight_head(base, c, 0, 0, wt_hi[:, c], D)
                if F["er"]:
                    weight_head(base, C, 0, 0, F["ag_hi"][:].rearrange("p c n -> p (c n)"), C * F["cols"])
                    weight_head(base, C + 1, 0, 0, F["lb_hi"][0:F["er"]], D, F["er"])

            def feed_forward(f):
                F, phase = FF[f], f"F{f}"
                er = F["er"]
                for s in range(B + 5):
                    if 2 <= s <= B + 1:
                        norm_head(phase, s - 2)
                    if er and 3 <= s <= B + 2:
                        b = s - 3
                        act.wait_ge(f_nmax, FM[f] + b + 1)
                        e = act.activation(gt[:, 0], ps[:, 2 + b % 2, er:er + NE], ACT.Exp, bias=thr[:, 0:1],
                                           accum_out=thr[:, 1:2])
                        if f == 3:
                            e = act.activation(thr[:, 2:3], ps[:, 2 + b % 2, er + NE:er + NE + 1], ACT.Exp,
                                               bias=thr[:, 3:4], scale=-1.0)
                        e.then_inc(f_exp, 1)
                    if er and 4 <= s <= B + 3:
                        b = s - 4
                        act.wait_ge(f_t, FM[f] + b + 1)
                        act.copy(hwt_hi[0:er], ps[0:er, 2 + b % 2, 256:384]).then_inc(f_thead, 1)

            def l1_keys():
                for b in range(B):
                    act.wait_ge(k_nmax, b + 1)
                    act.activation(probs[:, 0:D], cn_raw[:, b], ACT.Exp, bias=negmax[:, b % 2, 0:1],
                                   accum_out=sums[:, b % 2, 0:1]).then_inc(k_exp, 1)
                    act.wait_ge(k_t, b + 1)
                    act.copy(kt_hi[:], ps[:, 0, :].rearrange("p (c k) -> p c k", c=C)).then_inc(k_head, 1)
                    act.wait_ge(k_kvs, b + 1)
                    act.copy(kvs_hi[:, b], kvs[:]).then_inc(k_kvhead, 1)

            def l1_attention():
                for b in range(B):
                    act.wait_ge(ln_xn, LN["A1"] + b + 1)
                    if b >= 1:
                        act.wait_ge(a_done, b)
                        act.wait_ge(a_mm, b)
                    act.activation(probs[:, 0:D], xn[:, b % 2], ACT.Exp).then_inc(a_exp, 1)
                    act.wait_ge(a_exp, b + 1)
                    act.copy(ot_hi[:], probs[:, 0:D]).then_inc(a_head, 1)

            act.wait_ge(g_in, 32)
            act.activation(tg[:], gates[:], ACT.Tanh).then_inc(g_tanh, 1)
            act.mul(thr[:, 3:4], bthr[:], -1.0).then_inc(g_tanh, 1)
            act.wait_ge(g_tanh, 2)
            for b in range(B):
                norm_head("A0", b)
            act.wait_ge(ct_in, 16 * C)
            for c in range(C):
                act.copy(ct_hi[:, c], ct_raw[:, c]).then_inc(ct_head, 1)
            attention(Lq[0], "A0")
            ff_weights(0)
            feed_forward(0)
            l1_keys()
            act.wait_ge(tab_in, 16)
            act.copy(tab_hi[:], tab_raw[:]).then_inc(tab_head, 1)
            l1_attention()
            ff_weights(1)
            feed_forward(1)
            for b in range(B):
                norm_head("A2", b)
            attention(Lq[1], "A2")
            ff_weights(2)
            feed_forward(2)
            for b in range(B):
                norm_head("A3", b)
            attention(Lq[2], "A3")
            ff_weights(3)
            feed_forward(3)

        @block.gpsimd
        def _(gp):
            def norm_rstd(phase, b):
                n = LN[phase] + b
                gp.wait_ge(ln_var, n + 1)
                if n >= 2:
                    gp.wait_ge(ln_xn, n - 1)
                gp.tensor_tensor(rstd[:, b % 2:b % 2 + 1], ve[:, b % 2:b % 2 + 1], minus_half[:],
                                 ALU.pow).then_inc(ln_rstd, 1)

            def weight_tail(base, n_static, per_loop, i, lo, hi, cols, parts=P):
                k = base + n_static
                gp.wait_ge(w_head, k + 1 + per_loop * i)
                gp.tensor_tensor(lo, raw[0:parts, k % RAW, 0:cols], hi, ALU.subtract).then_inc(w_done, 1)

            def attention(L, phase):
                base, hd = W_BASE[phase], L.hd

                def proj_weight(t, i, n_static, per_loop):
                    lo, hi = {0: (L.wq_lo[:, 0], L.wq_hi[:, 0]), 1: (L.wkv_lo[:, 0], L.wkv_hi[:, 0]),
                              2: (L.wq_lo[:, 1], L.wq_hi[:, 1]), 3: (L.wkv_lo[:, 1], L.wkv_hi[:, 1]),
                              4: (L.wq_lo[:, 2], L.wq_hi[:, 2]), 5: (L.wq_lo[:, 3], L.wq_hi[:, 3])}[t]
                    weight_tail(base, n_static, per_loop, i, lo.rearrange("p c d -> p (c d)"),
                                hi.rearrange("p c d -> p (c d)"), C * hd)

                def rotated(b, k, i, when):
                    return L.index("KQ", i, b, k, when), L.index("KQ", 0, b, k, when) % 2

                def add_up(b, k, i, when=NOW):
                    m, a = rotated(b, k, i, when)
                    gp.wait_ge(L.s_rope, m + 1)
                    gp.tensor_tensor(rope_a[:, a], rope_a[:, a], rope_b[:], ALU.add).then_inc(L.s_rsum, 1)

                def tail(b, k, i, when=NOW):
                    m, a = rotated(b, k, i, when)
                    kind, n = L.fill[b][k]
                    half = L.half[b]
                    if kind == "K":
                        lo, hi = (w[:, half * HALF:(half + 1) * HALF, n].rearrange("p b t -> p (b t)")
                                  for w in (L.k_lo, L.k_hi))
                    else:
                        lo, hi = (w[:, n, half * HALF * P:(half + 1) * HALF * P] for w in (L.q_lo, L.q_hi))
                    gp.wait_ge(L.s_qk_head, m + 1)
                    gp.tensor_tensor(lo, rope_a[:, a], hi, ALU.subtract).then_inc(L.s_qk, 1)

                def normalise(b, i):
                    gp.wait_ge(L.s_rs, B * i + b + 1)
                    pv = probs[:, 0:GH * L.keys].rearrange("p (h k) -> p h k", h=GH)
                    gp.tensor_tensor(pv, pv, rsums[:, b % 2].unsqueeze(2).to_broadcast([P, GH, L.keys]),
                                     ALU.mult).then_inc(L.s_p, 1)

                def group(i, last):
                    for b in range(B):
                        late = L.rope and (b == 0 or not last or b <= 3)
                        pb = (b - 1) % 8
                        if late:
                            add_up(pb, len(L.fill[pb]) - 1, i, NOW if b else BEFORE)
                        normalise(b, i)
                        if late:
                            tail(pb, len(L.fill[pb]) - 1, i, NOW if b else BEFORE)
                        if L.rope and (not last or b < 3) and len(L.fill[b]) == 2 and L.fill[b][0][0] != "V":
                            add_up(b, 0, i)
                            tail(b, 0, i)
                        if b == 0:
                            for h in range(GH):
                                weight_tail(base, 6 + h, 10, i, L.wo_lo[0:hd, h], L.wo_hi[0:hd, h], D, hd)
                        elif not last:
                            for t in SPLIT_AT.get(b, []):
                                proj_weight(t, i, 10 + t, 10)

                for t in range(6):
                    proj_weight(t, 0, t, 0)
                if L.rope:
                    for b in range(3, 8):
                        for k, (kind, _) in enumerate(L.fill[b]):
                            if kind != "V" and (b, k) != (7, len(L.fill[7]) - 1):
                                add_up(b, k, 0, PROLOGUE)
                                tail(b, k, 0, PROLOGUE)
                with gp.Fori(0, L.groups - 1) as i:
                    group(i, False)
                group(L.groups - 1, True)

            def ff_weights(f):
                F, base = FF[f], W_BASE[f"F{f}"]
                for c in range(C):
                    weight_tail(base, c, 0, 0, wt_lo[:, c], wt_hi[:, c], D)
                if F["er"]:
                    weight_tail(base, C, 0, 0, F["ag_lo"][:].rearrange("p c n -> p (c n)"),
                                F["ag_hi"][:].rearrange("p c n -> p (c n)"), C * F["cols"])
                    weight_tail(base, C + 1, 0, 0, F["lb_lo"][0:F["er"]], F["lb_hi"][0:F["er"]], D, F["er"])

            def feed_forward(f):
                phase = f"F{f}"
                for b in range(B):
                    norm_rstd(phase, b)
                    if f >= 1 and b >= 1:
                        add_bias(f, b - 1)
                if f >= 1:
                    add_bias(f, B - 1)

            def add_bias(f, b):
                if b == 0:
                    gp.wait_ge(b_tg, FB[f] + 1)
                gp.wait_ge(ln_xn, LN[f"F{f}"] + b + 1)
                gp.tensor_tensor(x[:, b], x[:, b], bias[:], ALU.add).then_inc(b_x, 1)

            gp.wait_ge(cst, 1)
            for b in range(B):
                norm_rstd("A0", b)
            attention(Lq[0], "A0")
            ff_weights(0)
            feed_forward(0)
            for b in range(B):
                norm_rstd("A1", b)
            ff_weights(1)
            feed_forward(1)
            for b in range(B):
                norm_rstd("A2", b)
            attention(Lq[1], "A2")
            ff_weights(2)
            feed_forward(2)
            for b in range(B):
                norm_rstd("A3", b)
            attention(Lq[2], "A3")
            ff_weights(3)
            feed_forward(3)


def shape_constants():
    import numpy as _np
    f = _np.float32
    consts = _np.zeros((P, 2 * P + NE + C), f)
    consts[:, 0:P] = _np.eye(P)
    consts[:, P:2 * P] = _np.kron(_np.eye(P // 16), _np.ones((16, 16)))
    consts[:, 2 * P:2 * P + NE] = _np.arange(NE, 0, -1)
    consts[:, 2 * P + NE:] = _np.arange(P)[:, None] + P * _np.arange(C)[None, :]
    inv = (f(1.0) / _np.power(f(10000.0), _np.arange(0, P, 2, dtype=f) / f(P))).astype(f)
    ang = (_np.arange(C * P, dtype=f)[:, None] * inv[None, :]).astype(f)
    cos = _np.concatenate([_np.cos(ang), _np.cos(ang)], 1).astype(f)
    sin = _np.concatenate([-_np.sin(ang), _np.sin(ang)], 1).astype(f)
    rope2 = _np.stack([cos, sin], 1).reshape(C, P, 2, P).transpose(1, 0, 2, 3)
    rope3 = _np.stack([cos[:P].T, sin[:P].T], 1)
    n = D
    t = _np.arange(n)
    four = _np.zeros((n, n))
    four[0] = 1.0 / _np.sqrt(n)
    four[n - 1] = _np.where(t % 2 == 0, 1.0, -1.0) / _np.sqrt(n)
    for k in range(1, (n - 1) // 2 + 1):
        four[2 * k - 1] = _np.sqrt(2.0 / n) * _np.cos(2 * _np.pi * k * t / n)
        four[2 * k] = _np.sqrt(2.0 / n) * _np.sin(2 * _np.pi * k * t / n)
    fourier = four.astype(f).reshape(C, P, n).transpose(1, 0, 2)
    causal = _np.tril(_np.ones((P, P), f))
    return dict(consts=consts, rope2=rope2, rope3=rope3, fourier=fourier, causal=causal)


def kernel(**inputs):
    import numpy as _np
    import concourse.bacc as _bacc
    from concourse import mybir as _mybir
    from concourse.bass_utils import run_bass_kernel_spmd as _run

    a = {k: _np.asarray(v) for k, v in inputs.items()}

    def proj_tiles(wq, wk, wv, hd, groups):
        q = wq.reshape(C, P, groups, GH, hd).transpose(2, 3, 1, 0, 4).reshape(groups, GH, P, C * hd)
        k = wk.reshape(C, P, groups, hd).transpose(2, 1, 0, 3).reshape(groups, 1, P, C * hd)
        v = wv.reshape(C, P, groups, hd).transpose(2, 1, 0, 3).reshape(groups, 1, P, C * hd)
        return _np.concatenate([q[:, 0:1], k, q[:, 1:2], v, q[:, 2:4]], 1)

    def chunked(w):
        return w.reshape(C, P, -1).transpose(1, 0, 2).reshape(P, -1)

    arr = dict(shape_constants())
    arr["x"] = a["x"]
    arr["ctx"] = a["ctx_4096"].transpose(1, 0, 2)
    arr["ctx_t"] = a["ctx_4096"].reshape(T, C, P).transpose(1, 2, 0)
    arr["pos"] = a["pos_BxS2"].reshape(1, T)
    arr["mask"] = a["mask_BxSxS2_ik0"].transpose(1, 0, 2)
    arr["gates"] = _np.stack([a["g_xattn"], a["g_ffn"]], 1).reshape(1, 8)
    arr["b_thr"] = a["L3_ffn_b_thr"].reshape(1, 1)
    arr["L0_proj"] = proj_tiles(a["L0_xattn_Wq"].T, a["L0_xattn_Wk"].T, a["L0_xattn_Wv"].T, 96, 4)
    arr["L0_out"] = a["L0_xattn_Wo"].T.reshape(4, GH, 96, D)
    arr["L2_proj"] = proj_tiles(a["L2_xattn_Wq"], a["L2_xattn_Wk"], a["L2_xattn_Wv"], 128, 8)
    arr["L2_out"] = a["L2_xattn_Wo"].reshape(8, GH, 128, D)
    arr["L3_proj"] = proj_tiles(a["L3_xattn_Wq"].T, a["L3_xattn_Wk"].T, a["L3_xattn_Wv"].T, 128, 8)
    arr["L3_out"] = a["L3_xattn_Wd"].T.reshape(8, GH, 128, D)
    for f in range(4):
        arr[f"F{f}_w"] = a[f"L{f}_ffn_W_base"].T.reshape(C, P, D)
        if f >= 1:
            arr[f"F{f}_bias"] = a[f"L{f}_ffn_b_base"].reshape(1, D)
    lora = {0: ("L0_ffn_A", "L0_ffn_gate_W", "L0_ffn_B"), 2: ("L2_ffn_lora_A", "L2_ffn_W_router", "L2_ffn_lora_B"),
            3: ("L3_ffn_A_w", "L3_ffn_W_gate", "L3_ffn_B_w")}
    for f, (la, lg, lb) in lora.items():
        cols = [a[la].reshape(-1, D).T, a[lg].T]
        if f == 3:
            cols += [a["L3_ffn_W_thr"].reshape(D, 1)] * 2
        arr[f"F{f}_ag"] = chunked(_np.concatenate(cols, 1))
        arr[f"F{f}_b"] = a[lb].transpose(0, 2, 1).reshape(-1, D)
    rows = lambda w: w.reshape(3, C, P, -1).transpose(2, 1, 0, 3)
    arr["F1_coef"] = _np.concatenate([rows(a["L1_ffn_coefs0"]), rows(a["L1_ffn_coefs1"])], 3)
    arr["F1_mask"] = _np.concatenate([rows(a["L1_ffn_mask0"]), rows(a["L1_ffn_mask1"])], 3).astype(_np.int32)
    arr["F1_enc"] = _np.concatenate([a["L1_ffn_enc0"], a["L1_ffn_enc1"]], 0)

    nc = _bacc.Bacc("TRN2", target_bir_lowering=False, num_devices=1, dynamic_dma_scratch_size=256)
    feed, aps = {}, {}
    for name, w in arr.items():
        w = _np.ascontiguousarray(w)
        feed[f"in_{name}"] = w
        aps[name] = nc.dram_tensor(f"in_{name}", w.shape, _mybir.dt.from_np(w.dtype), kind="ExternalInput").ap()
    out = nc.dram_tensor("out_0", (B, P, D), _mybir.dt.float32, kind="ExternalOutput").ap()
    build(nc, aps, out)
    r = _run(nc, [feed], core_ids=[0])
    return r.results[0]["out_0"]
```

```python
from contextlib import ExitStack

import numpy as np

import concourse.bass as bass
from concourse import mybir
from concourse.alu_op_type import AluOpType as ALU

F32 = mybir.dt.float32
F32R = mybir.dt.float32r
I32 = mybir.dt.int32
U8 = mybir.dt.uint8
ACT = mybir.ActivationFunctionType
X_AXIS = mybir.AxisListType.X

B, P, D = 8, 128, 512
T = B * P
C = D // P
HALF = 4
GH = 4
NE = 8
RAW = 5
RAW_COLS = C * (P + NE + 2)
LN_EPS = 1e-5

FILL_ROPE = {3: [("K", 0), ("Q", 0)], 4: [("Q", 1), ("W", 0)], 5: [("V", 0), ("Q", 2)], 6: [("Q", 3)]}
FILL_TWO = {3: [("K", 0), ("Q", 0)], 4: [("Q", 1), ("W", 0)], 5: [("V", 0), ("K", 1), ("Q", 2)],
            6: [("W", 1), ("Q", 3), ("V", 1)]}
WEIGHT_ORDER = {("Q", 0): 0, "K": 1, ("Q", 1): 2, "W": 3, ("Q", 2): 4, ("Q", 3): 5}
SPLIT_AT = {1: [0], 2: [1, 2], 3: [3, 4], 4: [5]}


FF_START = {0: 5, 1: 0, 2: 5, 3: 5}
FF_NEXT = {1: "A2", 2: "A3"}

PROLOGUE, NOW, BEFORE = range(3)


class Layer:

    def __init__(self, name, groups, hd, sources, rope, gate):
        self.name, self.groups, self.hd, self.sources, self.rope, self.gate = name, groups, hd, sources, rope, gate
        fill = FILL_TWO if sources == 2 else FILL_ROPE
        self.fill = {b: fill[b if 3 <= b <= 6 else (b - 4) % 8] for b in range(8)}
        self.half = {b: 0 if 3 <= b <= 6 else 1 for b in range(8)}
        self.scale = float(hd) ** -0.5
        self.keys = sources * P
        self.weight_tiles = 10 * groups
        self.first = {b: sum(len(self.fill[k]) for k in range(3, b)) for b in range(3, 9)}
        self.off = {b: self.first[8] + sum(len(self.fill[k]) for k in range(b)) for b in range(8)}
        self.per_group = sum(len(f) for f in self.fill.values())
        self.tiles = self.first[8] + self.per_group * (groups - 1) + sum(len(self.fill[k]) for k in range(3))

    def kinds(self, want, b, pro):
        n = lambda k: sum(1 for kind, _ in self.fill[k] if kind in want)
        if pro:
            return sum(n(k) for k in range(3, b))
        return sum(n(k) for k in range(3, 8)) + sum(n(k) for k in range(b))

    def kinds_group(self, want):
        return sum(1 for f in self.fill.values() for kind, _ in f if kind in want)

    def index(self, want, g, b, k, when=NOW):
        inside = sum(1 for kind, _ in self.fill[b][:k] if kind in want)
        base = self.kinds(want, b, when != NOW) + inside
        return base if when == PROLOGUE else self.kinds_group(want) * g + base

    def tile(self, g, b, k, when=NOW):
        base = (self.off[b] if when == NOW else self.first[b]) + k
        return (base if when == PROLOGUE else self.per_group * g + base), base % 2

    def two_before(self, b, k, when):
        steps = range(3, 8) if when == PROLOGUE else range(8)
        seq = [(s, j) for s in steps for j in range(len(self.fill[s]))]
        n = seq.index((b, k)) - 2
        if n >= 0:
            return seq[n] + (when,)
        if when == PROLOGUE:
            return None
        seq = [(s, j) for s in range(3, 8) for j in range(len(self.fill[s]))]
        return seq[n] + (BEFORE,)

    def ready(self, want, g, half):
        if half == 1:
            return g * self.kinds_group(want) + self.kinds(want, 3, False)
        return g * self.kinds_group(want) + self.kinds(want, 7, True)


def build(nc, inp, out):
    ctx = ExitStack()
    with ctx:
        sem = lambda name: ctx.enter_context(nc.semaphore(name))

        cursor = [384]

        def region(size):
            at = cursor[0]
            cursor[0] += (size + 31) // 32 * 32
            return at

        def at(name, shape, dt, offset):
            return nc.alloc_sbuf_tensor_at(name, shape, dt, offset=offset)

        def new(name, shape, dt):
            size = int(np.prod(shape[1:])) * (1 if dt == U8 else 4)
            return at(name, shape, dt, region(size))

        x = new("x", [P, B, D], F32)
        r_xt = region(2 * 16384)
        xt_hi = at("xt_hi", [P, C, T], F32R, r_xt)
        xt_lo = at("xt_lo", [P, C, T], F32R, r_xt + 16384)
        ct_hi = new("ct_hi", [P, C, T], F32R)
        ct_lo = new("ct_lo", [P, C, T], F32R)
        r_wq, r_wkv, r_wo = region(16384), region(8192), region(16384)
        r_q, r_k, r_v, r_pt = region(32768), region(16384), region(12288), region(10240)
        raw = new("raw", [P, RAW, RAW_COLS], F32)
        probs = new("probs", [P, GH * 2 * P], F32)
        ot_hi = new("ot_hi", [P, GH * P], F32R)
        ot_lo = new("ot_lo", [P, GH * P], F32R)
        vt = new("vt", [P, HALF * P], F32)
        xn = new("xn", [P, 2, D], F32)
        bias = new("bias", [P, D], F32)
        consts = new("consts", [P, 2 * P + NE + C], F32)
        ident, blk = consts[:, 0:P], consts[:, P:2 * P]
        iota8, pidx = consts[:, 2 * P:2 * P + NE], consts[:, 2 * P + NE:]
        kc = new("kc", [P, B, 16], F32)
        gates = new("gates", [P, 8], F32)
        tg = new("tg", [P, 8], F32)
        stats = new("stats", [P, 2, 6], F32)
        mv = new("mv", [P, 2, 2], F32)
        ve = new("ve", [P, 2], F32)
        rstd = new("rstd", [P, 2], F32)
        minus_half = new("minus_half", [P, 1], F32)
        fill = new("fill", [P, 2], F32)
        negmax = new("negmax", [P, 2, GH], F32)
        nbias = new("nbias", [P, 2, GH], F32)
        sums = new("sums", [P, 2, GH], F32)
        rsums = new("rsums", [P, 2, GH], F32)
        gt = new("gt", [P, 16, NE], F32)
        thr = new("thr", [P, 8], F32)
        bthr = new("bthr", [P, 1], F32)
        assert cursor[0] <= nc.sbuf_usable_end

        Lq = [Layer("L0", 4, 96, 2, False, 0), Layer("L2", 8, 128, 1, True, 4), Layer("L3", 8, 128, 1, True, 6)]
        for L in Lq:
            n, hd, s = L.name, L.hd, L.sources
            kv = B * s * P * 4
            vb = B * s * hd * 4
            L.wq_hi = at(f"wq_hi{n}", [P, GH, C, hd], F32R, r_wq)
            L.wq_lo = at(f"wq_lo{n}", [P, GH, C, hd], F32R, r_wq + 8192)
            L.wkv_hi = at(f"wkv_hi{n}", [P, 2, C, hd], F32R, r_wkv)
            L.wkv_lo = at(f"wkv_lo{n}", [P, 2, C, hd], F32R, r_wkv + 4096)
            L.wo_hi = at(f"wo_hi{n}", [P, GH, D], F32R, r_wo)
            L.wo_lo = at(f"wo_lo{n}", [P, GH, D], F32R, r_wo + 8192)
            L.q_hi = at(f"q_hi{n}", [P, GH, T], F32R, r_q)
            L.q_lo = at(f"q_lo{n}", [P, GH, T], F32R, r_q + 16384)
            L.k_hi = at(f"k_hi{n}", [P, B, s, P], F32R, r_k)
            L.k_lo = at(f"k_lo{n}", [P, B, s, P], F32R, r_k + kv)
            L.v_hi = at(f"v_hi{n}", [P, B, s, hd], F32R, r_v)
            L.v_lo = at(f"v_lo{n}", [P, B, s, hd], F32R, r_v + vb)
            L.pt_hi = at(f"pt_hi{n}", [P, s, GH * P], F32R, r_pt)
            L.pt_lo = at(f"pt_lo{n}", [P, s, GH * P], F32R, r_pt + s * 2048)
        rope_a = at("rope_a", [P, 2, D], F32, r_pt + 4096)
        rope_b = at("rope_b", [P, D], F32, r_pt + 8192)
        cos2 = at("cos2", [P, T], F32, r_k + 8192)
        sin2 = at("sin2", [P, T], F32, r_k + 12288)
        rot3 = at("rot3", [P, 2, P], F32, r_k + 8192)
        mask2 = at("mask2", [P, B, P], U8, r_v + 8192)
        mask3 = at("mask3", [P, 1, P], U8, r_v + 8192 + 1024)
        causal = at("causal", [P, P], F32, r_v + 8192 + 1280)
        mask_in = at("mask_in", [P, B, P], I32, r_v)
        wt_hi = at("wt_hi", [P, C, D], F32R, r_wq)
        wt_lo = at("wt_lo", [P, C, D], F32R, r_wq + 8192)
        FF = []
        for f, er, extra in ((0, 64, 0), (1, 0, 0), (2, 128, 0), (3, 128, 2)):
            n = er + NE + extra
            FF.append(dict(
                f=f, er=er, cols=n,
                ag_hi=at(f"ag_hi{f}", [P, C, n], F32R, r_q) if er else None,
                ag_lo=at(f"ag_lo{f}", [P, C, n], F32R, r_q + 2304) if er else None,
                lb_hi=at(f"lb_hi{f}", [P, D], F32R, r_q + 4608) if er else None,
                lb_lo=at(f"lb_lo{f}", [P, D], F32R, r_q + 6656) if er else None))
        hw = at("hw", [P, 2, P], F32, r_q + 8704)
        hwt_hi = at("hwt_hi", [P, P], F32R, r_q + 9728)
        hwt_lo = at("hwt_lo", [P, P], F32R, r_q + 10240)
        ct_raw = at("ct_raw", [P, C, T], F32, r_q + 16384)
        cn_raw = at("cn_raw", [P, B, D], F32, r_wo)
        kt_hi = at("kt_hi", [P, 2, C, P], F32R, r_pt)
        kt_lo = at("kt_lo", [P, 2, C, P], F32R, r_pt + 4096)
        kvm = at("kvm", [P, P], F32, r_pt + 8192)
        e_hi = at("e_hi", [P, B, D], F32R, r_xt)
        e_lo = at("e_lo", [P, B, D], F32R, r_xt + 16384)
        kvs = at("kvs", [P, B, P], F32, r_pt)
        sel_in = at("sel_in", [P, B, B * 8], F32, r_pt + 4096)
        spread_in = at("spread_in", [B * 8, B, P], F32, r_pt + 6144)
        kvs_hi = at("kvs_hi", [P, B, P], F32R, r_k)
        kvs_lo = at("kvs_lo", [P, B, P], F32R, r_k + 4096)
        sel = at("sel", [P, B, B * 8], F32R, r_wkv)
        spread = at("spread", [B * 8, B, P], F32R, r_wkv + 2048)
        tab_raw = at("tab_raw", [P, C, 2, P], F32, r_wo)
        tab_hi = at("tab_hi", [P, C, 2, P], F32R, r_wo + 4096)
        tab_lo = at("tab_lo", [P, C, 2, P], F32R, r_wo + 8192)
        pos_i = at("pos_i", [P, T], I32, r_wo + 12288)
        pos_f = at("pos_f", [P, T], F32, r_v)
        pos_n = at("pos_n", [P, T], F32, r_v + 4096)
        onehot = [at(f"onehot{c}", [P, T], F32R, place)
                  for c, place in enumerate((r_v + 4096, r_v + 8192, r_k + 8192, r_k + 12288))]
        four = at("four", [P, C, D], F32, r_q + 16384)
        cf_in = at("cf_in", [P, C, 3, 40], F32, r_q + 24576)
        cm_in = at("cm_in", [P, C, 3, 40], I32, r_q + 26496)
        cm_f = at("cm_f", [P, C, 3, 40], F32, r_q + 28416)
        ws = at("ws", [P, C, 40], F32, r_q + 30336)
        enc = at("enc", [40, D], F32, r_q + 10752)
        gk = at("gk", [40, D], F32, r_q + 12800)

        ps = ctx.enter_context(nc.psum_tensor("ps", [P, 8, 512], F32))
        S_BANK, T_BANK, O_BANK, Y_BANK = 2, 4, 6, 7

        for L in Lq:
            L.s_proj = sem(f"{L.name}_proj")
            L.s_rope = sem(f"{L.name}_rope") if L.rope else None
            L.s_rsum = sem(f"{L.name}_rsum") if L.rope else None
            L.s_qk_head = sem(f"{L.name}_qk_head")
            L.s_qk = sem(f"{L.name}_qk")
            L.s_w = sem(f"{L.name}_w")
            L.s_v_head = sem(f"{L.name}_v_head")
            L.s_v = sem(f"{L.name}_v")
            L.s_s = sem(f"{L.name}_s")
            L.s_seen = sem(f"{L.name}_seen") if L.rope else None
            L.s_smask = sem(f"{L.name}_smask") if L.rope else None
            L.s_smax = sem(f"{L.name}_smax")
            L.s_nb = sem(f"{L.name}_nb")
            L.s_e = sem(f"{L.name}_e")
            L.s_rs = sem(f"{L.name}_rs")
            L.s_p = sem(f"{L.name}_p")
            L.s_t = sem(f"{L.name}_t")
            L.s_pt_head = sem(f"{L.name}_pt_head")
            L.s_pt = sem(f"{L.name}_pt")
            L.s_o = sem(f"{L.name}_o")
            L.s_o_head = sem(f"{L.name}_o_head")
            L.s_ot = sem(f"{L.name}_ot")
            L.s_y = sem(f"{L.name}_y")
            L.s_x = sem(f"{L.name}_x")
        raw_in = [sem(f"raw_in{i}") for i in range(RAW)]
        w_head = sem("w_head")
        w_done = sem("w_done")
        x_in = [sem(f"x_in{j}") for j in range(B // 2)]
        ct_in, ct_head, ct_done = sem("ct_in"), sem("ct_head"), sem("ct_done")
        cst_in, cst, sel_dma, sel_done = sem("cst_in"), sem("cst"), sem("sel_dma"), sem("sel_done")
        g_in, g_tanh = sem("g_in"), sem("g_tanh")
        ln_var, ln_rstd, ln_xn = sem("ln_var"), sem("ln_rstd"), sem("ln_xn")
        ln_t, ln_head, ln_done = sem("ln_t"), sem("ln_head"), sem("ln_done")
        chain = sem("chain")
        pchain = sem("pchain")
        f_h, f_base, f_t, f_y = sem("f_h"), sem("f_base"), sem("f_t"), sem("f_y")
        f_nmax, f_exp, f_hw = sem("f_nmax"), sem("f_exp"), sem("f_hw")
        f_thead, f_tdone, f_x = sem("f_thead"), sem("f_tdone"), sem("f_x")
        b_in, b_tg, b_x = sem("b_in"), sem("b_tg"), sem("b_x")
        cn_in = [sem(f"cn_in{j}") for j in range(2)]
        k_nmax, k_exp, k_t, k_head, k_done = (sem("k_nmax"), sem("k_exp"), sem("k_t"),
                                                     sem("k_head"), sem("k_done"))
        k_kv, k_sum, k_kvs, k_kvhead, k_kvdone = sem("k_kv"), sem("k_sum"), sem("k_kvs"), sem("k_kvhead"), sem("k_kvdone")
        a_exp, a_head, a_done, a_den = sem("a_exp"), sem("a_head"), sem("a_done"), sem("a_den")
        a_rec, a_rhead, a_rdone = sem("a_rec"), sem("a_rhead"), sem("a_rdone")
        a_bc, a_num, a_copy, a_x = sem("a_bc"), sem("a_num"), sem("a_copy"), sem("a_x")
        tab_in, tab_head, tab_done, pos_in = sem("tab_in"), sem("tab_head"), sem("tab_done"), sem("pos_in")
        oh, oh_mm, rot_out = sem("oh"), sem("oh_mm"), sem("rot_out")
        four_in, ws_done, gk_mm, gk_done, we_mm, we_done = (sem("four_in"), sem("ws_done"), sem("gk_mm"),
                                                            sem("gk_done"), sem("we_mm"), sem("we_done"))
        m_in, m_done, rot3_in = sem("m_in"), sem("m_done"), sem("rot3_in")
        out_done = sem("out_done")

        order = []
        n = 0
        for phase, tiles in (("A0", Lq[0].weight_tiles), ("F0", 6), ("F1", C), ("A2", Lq[1].weight_tiles),
                             ("F2", 6), ("A3", Lq[2].weight_tiles), ("F3", 6)):
            order.append((phase, n, tiles))
            n += tiles
        W_BASE = {phase: first for phase, first, _ in order}
        LN = {"A0": 0, "F0": 8, "A1": 16, "F1": 24, "A2": 32, "F2": 40, "A3": 48, "F3": 56}
        LNT = {"A0": 0, "F0": 8, "F1": 16, "A2": 24, "F2": 32, "A3": 40, "F3": 48}
        FN = {0: 0, 1: 8, 2: 16, 3: 24}
        FM = {0: 0, 2: 8, 3: 16}
        FB = {1: 0, 2: 1, 3: 2}

        def slot(base, n_static, n):
            s = (base + n_static) % RAW
            return s, n

        def raw_ready(engine, base, n_static, per_loop, i):
            k = base + n_static
            engine.wait_ge(raw_in[k % RAW], 16 * (k // RAW + 1) + 16 * (per_loop // RAW) * i)
            return k % RAW

        def triple(pe, dst, l_hi, l_lo, r_hi, r_lo, start, stop):
            pe.matmul(dst, l_hi, r_hi, start=start, stop=False)
            pe.matmul(dst, l_hi, r_lo, start=False, stop=False)
            return pe.matmul(dst, l_lo, r_hi, start=False, stop=stop)

        block = ctx.enter_context(nc.Block())

        @block.sync
        def _(sp):
            def load_tile(base, n_static, per_loop, i, src, cols, parts=P):
                k = base + n_static
                if k >= RAW:
                    sp.wait_ge(w_done, k - RAW + 1 + per_loop * i)
                sp.dma_start(raw[0:parts, k % RAW, 0:cols], src).then_inc(raw_in[k % RAW], 16)

            def attention(L):
                base, wp, wo = W_BASE["A" + L.name[1]], inp[L.name + "_proj"], inp[L.name + "_out"]
                for t in range(6):
                    if L.name == "L0" and t == RAW:
                        for b in range(B):
                            sp.dma_start(cn_raw[:, b], inp["ctx"][b]).then_inc(cn_in[b // 4], 16)
                    load_tile(base, t, 0, 0, wp[0, t], C * L.hd)

                def group(i, last):
                    for h in range(GH):
                        load_tile(base, 6 + h, 10, i, wo[bass.ts(i, 1), h][0] if not isinstance(i, int) else wo[i, h],
                                  D, L.hd)
                    if not last:
                        for t in range(6):
                            load_tile(base, 10 + t, 10, i,
                                      wp[bass.ts(i + 1, 1), t][0] if not isinstance(i, int) else wp[i + 1, t],
                                      C * L.hd)
                with sp.Fori(0, L.groups - 1) as i:
                    group(i, False)
                group(L.groups - 1, True)

            def feed_forward(f):
                base = W_BASE[f"F{f}"]
                if f >= 1:
                    if f >= 2:
                        sp.wait_ge(b_x, B * (f - 1))
                    sp.dma_start(bias[:], inp[f"F{f}_bias"].broadcast_to([P, D])).then_inc(b_in, 16)
                for c in range(C):
                    load_tile(base, c, 0, 0, inp[f"F{f}_w"][c], D)
                if f != 1:
                    load_tile(base, C, 0, 0, inp[f"F{f}_ag"], C * FF[f]["cols"])
                    load_tile(base, C + 1, 0, 0, inp[f"F{f}_b"], D, FF[f]["er"])

            sp.dma_start(consts[:], inp["consts"]).then_inc(cst_in, 16)
            for b in range(B):
                sp.dma_start(x[:, b, :], inp["x"][b]).then_inc(x_in[b // 2], 16)
            sp.dma_start(gates[:], inp["gates"].broadcast_to([P, 8])).then_inc(g_in, 16)
            sp.dma_start(bthr[:], inp["b_thr"].broadcast_to([P, 1])).then_inc(g_in, 16)
            for c in range(C):
                sp.dma_start(ct_raw[:, c, :], inp["ctx_t"][c]).then_inc(ct_in, 16)
            attention(Lq[0])
            feed_forward(0)
            last = B * Lq[0].groups
            sp.wait_ge(Lq[0].s_y, last)
            sp.dma_start(tab_raw[:], inp["rope2"]).then_inc(tab_in, 16)
            sp.dma_start(pos_i[:], inp["pos"].broadcast_to([P, T])).then_inc(pos_in, 16)
            sp.dma_start(four[:], inp["fourier"]).then_inc(four_in, 16)
            sp.dma_start(cf_in[:], inp["F1_coef"]).then_inc(four_in, 16)
            sp.dma_start(cm_in[:], inp["F1_mask"]).then_inc(four_in, 16)
            sp.dma_start(enc[:], inp["F1_enc"]).then_inc(four_in, 16)
            sp.dma_start(sel_in[:], inp["sel"]).then_inc(sel_dma, 16)
            sp.dma_start(spread_in[:], inp["spread"]).then_inc(sel_dma, 16)
            feed_forward(1)
            sp.wait_ge(oh_mm, C)
            sp.dma_start(mask_in[:], inp["mask"]).then_inc(m_in, 16)
            sp.dma_start(causal[:], inp["causal"]).then_inc(m_in, 16)
            attention(Lq[1])
            feed_forward(2)
            sp.wait_ge(Lq[1].s_rope, Lq[1].ready("KQ", Lq[1].groups - 1, 1))
            sp.dma_start(rot3[:], inp["rope3"]).then_inc(rot3_in, 16)
            attention(Lq[2])
            feed_forward(3)
            for b in range(B):
                sp.wait_ge(f_x, FN[3] + b + 1)
                sp.dma_start(out[b], x[:, b, :]).then_inc(out_done, 16)
            sp.wait_ge(out_done, 16 * B)

        @block.tensor
        def _(pe):
            def norm_transpose(phase, b):
                n = LNT[phase] + b
                pe.wait_ge(ln_xn, LN[phase] + b + 1)
                if n >= 2:
                    pe.wait_ge(ln_done, n - 1)
                for c in range(C):
                    mm = pe.transpose(ps[:, b % 2, c * P:(c + 1) * P], xn[:, b % 2, c * P:(c + 1) * P], ident)
                mm.then_inc(ln_t, 1)

            def attention(L, phase):
                base, hd, after = W_BASE[phase], L.hd, "F" + phase[1]

                def fillers(b, i, when=NOW, only=None):
                    half = L.half[b]
                    tok = slice(half * HALF * P, (half + 1) * HALF * P)
                    ahead = 0 if when == PROLOGUE or b < 3 else 1
                    for k, (kind, n) in enumerate(L.fill[b]):
                        if only is not None and k != only:
                            continue
                        t, bank = L.tile(i, b, k, when)
                        last_user = L.two_before(b, k, when)
                        if last_user:
                            pb, pk, pw = last_user
                            if L.fill[pb][pk][0] == "V":
                                pe.wait_ge(L.s_v, L.index("V", i, pb, pk, pw) + 1)
                            elif L.fill[pb][pk][0] == "W":
                                pe.wait_ge(L.s_w, L.index("W", i, pb, pk, pw) + 1)
                            elif L.rope:
                                pe.wait_ge(L.s_rope, L.index("KQ", i, pb, pk, pw) + 1)
                            else:
                                pe.wait_ge(L.s_qk, L.index("KQ", i, pb, pk, pw) + 1)
                        if kind == "V":
                            pe.wait_ge(L.s_w, L.index("V", i, b, k, when) + 1)
                            for j in range(HALF):
                                mm = pe.transpose(ps[:, bank, j * hd:(j + 1) * hd], vt[0:hd, j * P:(j + 1) * P],
                                                  ident[0:hd, 0:hd])
                            mm.then_inc(L.s_proj, 1)
                            continue
                        w = WEIGHT_ORDER[(kind, n) if kind == "Q" else kind]
                        if when == PROLOGUE:
                            pe.wait_ge(w_done, base + w + 1)
                        else:
                            pe.wait_ge(w_done, (i + ahead) * 10 + (base + w + 1))
                        src_hi, src_lo = (xt_hi, xt_lo) if kind == "Q" or n == 1 else (ct_hi, ct_lo)
                        w_hi, w_lo = {"Q": (L.wq_hi[:, n], L.wq_lo[:, n]), "K": (L.wkv_hi[:, 0], L.wkv_lo[:, 0]),
                                      "W": (L.wkv_hi[:, 1], L.wkv_lo[:, 1])}[kind]
                        for c in range(C):
                            mm = triple(pe, ps[0:hd, bank, :], w_hi[:, c, :], w_lo[:, c, :],
                                        src_hi[:, c, tok], src_lo[:, c, tok], c == 0, c == C - 1)
                        mm.then_inc(L.s_proj, 1)

                def scores(b, i):
                    bank = S_BANK + (b % 2 if L.sources == 1 else 0)
                    pe.wait_ge(L.s_e, B * i + b + 1)
                    if b % HALF == 0:
                        pe.wait_ge(L.s_qk, L.ready("KQ", i, b // HALF))
                    for h in range(GH):
                        at_ = ps[:, bank + h * L.keys // 512, (h * L.keys) % 512:(h * L.keys) % 512 + L.keys]
                        mm = triple(pe, at_, L.q_hi[0:hd, h, b * P:(b + 1) * P], L.q_lo[0:hd, h, b * P:(b + 1) * P],
                                    L.k_hi[0:hd, b].rearrange("p s k -> p (s k)"),
                                    L.k_lo[0:hd, b].rearrange("p s k -> p (s k)"), True, True)
                    mm.then_inc(L.s_s, 1)

                def transposes(b, i):
                    pe.wait_ge(L.s_p, B * i + b + 1)
                    for h in range(GH):
                        for s in range(L.sources):
                            at_ = (h * L.sources + s) * P
                            mm = pe.transpose(ps[:, T_BANK + s, h * P:(h + 1) * P], probs[:, at_:at_ + P], ident)
                    mm.then_inc(L.s_t, 1)

                def heads_out(b, i):
                    pe.wait_ge(L.s_pt, B * i + b + 1)
                    if b % HALF == 0:
                        pe.wait_ge(L.s_v, L.ready("V", i, b // HALF))
                    for s in range(L.sources):
                        mm = triple(pe, ps[0:hd, O_BANK, :], L.v_hi[:, b, s], L.v_lo[:, b, s],
                                    L.pt_hi[:, s], L.pt_lo[:, s], s == 0, s == L.sources - 1)
                    mm.then_inc(L.s_o, 1)

                def out_proj(b, i):
                    pe.wait_ge(L.s_ot, B * i + b + 1)
                    pe.wait_ge(L.s_x, B * i + b + 1)
                    if b == 0:
                        pe.wait_ge(w_done, base + 10 + 10 * i)
                    for h in range(GH):
                        mm = triple(pe, ps[:, Y_BANK, :], ot_hi[0:hd, h * P:(h + 1) * P],
                                    ot_lo[0:hd, h * P:(h + 1) * P], L.wo_hi[0:hd, h], L.wo_lo[0:hd, h],
                                    h == 0, h == GH - 1)
                    mm.then_inc(L.s_y, 1)

                def group(i, last):
                    for b in range(B):
                        if b == 1:
                            transposes(0, i)
                        scores(b, i)
                        if b >= 2:
                            transposes(b - 1, i)
                        if b >= 2:
                            out_proj(b - 2, i)
                        if b >= 1:
                            heads_out(b - 1, i)
                        if last and b >= 5:
                            norm_transpose(after, b - 5)
                        if b < 3 or (not last and b < B - 1):
                            fillers(b, i)
                    if not last:
                        fillers(B - 1, i, only=0)
                    transposes(B - 1, i)
                    out_proj(B - 2, i)
                    heads_out(B - 1, i)
                    if not last:
                        fillers(B - 1, i, only=1)
                    out_proj(B - 1, i)
                    if last:
                        norm_transpose(after, B - 5)

                n = 0
                for b in range(3, 8):
                    for k in range(len(L.fill[b])):
                        if phase == "A0":
                            l1_keys(n)
                        fillers(b, 0, PROLOGUE, only=k)
                        n += 1
                if phase == "A0":
                    pe.wait_ge(k_sum, B)
                with pe.Fori(0, L.groups - 1) as i:
                    group(i, False)
                group(L.groups - 1, True)

            def feed_forward(f):
                F, base = FF[f], W_BASE[f"F{f}"]
                er, phase = F["er"], f"F{f}"

                def products(b):
                    rows = slice(b * P, (b + 1) * P)
                    pe.wait_ge(ln_done, LNT[phase] + b + 1)
                    if b == 0:
                        pe.wait_ge(w_done, base + (C + 2 if er else C))
                    if er:
                        if b >= 2:
                            pe.wait_ge(f_tdone, FM[f] + b - 1)
                        for c in range(C):
                            mm = triple(pe, ps[:, 2 + b % 2, 0:F["cols"]], xt_hi[:, c, rows], xt_lo[:, c, rows],
                                        F["ag_hi"][:, c], F["ag_lo"][:, c], c == 0, c == C - 1)
                        mm.then_inc(f_h, 1)
                    if b >= 4:
                        pe.wait_ge(f_x, FN[f] + b - 3)
                    for c in range(C):
                        mm = triple(pe, ps[:, 4 + b % 4, :], xt_hi[:, c, rows], xt_lo[:, c, rows],
                                    wt_hi[:, c], wt_lo[:, c], c == 0, c == C - 1 and not er)
                    if not er:
                        mm.then_inc(f_y, 1)

                def experts(b):
                    pe.wait_ge(f_hw, FM[f] + b + 1)
                    pe.transpose(ps[0:er, 2 + b % 2, 256:384], hw[:, b % 2, 0:er], ident).then_inc(f_t, 1)
                    pe.wait_ge(f_tdone, FM[f] + b + 1)
                    triple(pe, ps[:, 4 + b % 4, :], hwt_hi[0:er], hwt_lo[0:er], F["lb_hi"][0:er], F["lb_lo"][0:er],
                           False, True).then_inc(f_y, 1)

                for s in range(FF_START[f], B + 12 if f in FF_NEXT else B + 7):
                    if 1 <= s <= B:
                        norm_transpose(phase, s - 1)
                    if er and 7 <= s < B + 7:
                        experts(s - 7)
                    if 5 <= s < B + 5:
                        products(s - 5)
                    if f in FF_NEXT and s >= 11 and s < B + 11:
                        norm_transpose(FF_NEXT[f], s - 11)

            def l1_keys(s):
                if s <= B:
                    if s < B:
                        b = s
                        pe.wait_ge(k_exp, b + 1)
                        if b >= 2:
                            pe.wait_ge(k_done, b - 1)
                        for c in range(C):
                            mm = pe.transpose(ps[:, 2 + b % 2, c * P:(c + 1) * P],
                                              probs[:, b % 2 * D + c * P:b % 2 * D + (c + 1) * P], ident)
                        mm.then_inc(k_t, 1)
                    if s >= 1:
                        b = s - 1
                        pe.wait_ge(k_done, b + 1)
                        if b >= 2:
                            pe.wait_ge(k_sum, b - 1)
                        for c in range(C):
                            mm = triple(pe, ps[:, 4 + b % 2, 0:P], kt_hi[:, b % 2, c], kt_lo[:, b % 2, c],
                                        ct_hi[:, c, b * P:(b + 1) * P], ct_lo[:, c, b * P:(b + 1) * P],
                                        c == 0, c == C - 1)
                        mm.then_inc(k_kv, 1)

            def l1_denominators():
                pe.wait_ge(sel_done, 1)
                for b in range(B):
                    pe.wait_ge(a_done, b + 1)
                    pe.matmul(ps[0:B * 8, 2, :], sel[:, b], e_hi[:, b], start=b == 0, stop=False)
                    mm = pe.matmul(ps[0:B * 8, 2, :], sel[:, b], e_lo[:, b], start=False, stop=b == B - 1)
                mm.then_inc(a_den, 1)

            def l1_attention():
                pe.wait_ge(sel_done, 2)
                pe.wait_ge(a_rdone, 1)
                pe.wait_ge(k_kvdone, 1)
                for b in range(B):
                    if b >= 2:
                        pe.wait_ge(a_copy, b - 1)
                    pe.matmul(ps[:, b % 2, :], spread[:, b], ot_hi[0:B * 8], start=True, stop=False)
                    pe.matmul(ps[:, b % 2, :], spread[:, b], ot_lo[0:B * 8], start=False,
                              stop=True).then_inc(a_bc, 1)
                    if b >= 2:
                        pe.wait_ge(a_x, b - 1)
                    triple(pe, ps[:, 2 + b % 2, :], kvs_hi[:, b], kvs_lo[:, b], e_hi[:, b], e_lo[:, b],
                           True, True).then_inc(a_num, 1)

            def rope_tables():
                pe.wait_ge(tab_done, 1)
                for c in range(C):
                    pe.wait_ge(oh, c + 1)
                    for t in range(2):
                        for half in range(2):
                            bank, tok = 4 + 2 * t + half, slice(half * 512, (half + 1) * 512)
                            pe.matmul(ps[:, bank, :], tab_hi[:, c, t], onehot[c][:, tok], start=c == 0, stop=False)
                            mm = pe.matmul(ps[:, bank, :], tab_lo[:, c, t], onehot[c][:, tok], start=False,
                                           stop=c == C - 1)
                    mm.then_inc(oh_mm, 1)

            def l1_coefficients():
                pe.wait_ge(four_in, 64)
                pe.wait_ge(ws_done, 1)
                for c in range(C):
                    mm = pe.matmul(ps[0:40, 0, :], ws[:, c], four[:, c], start=c == 0, stop=c == C - 1)
                mm.then_inc(gk_mm, 1)

            def l1_weight():
                pe.wait_ge(gk_done, 1)
                for c in range(C):
                    pe.matmul(ps[:, 4 + c, :], enc[:, c * P:(c + 1) * P], gk[:], start=True,
                              stop=True).then_inc(we_mm, 1)

            pe.wait_ge(cst_in, 16)
            for b in range(B):
                norm_transpose("A0", b)
            pe.wait_ge(ct_done, C)
            pe.wait_ge(ln_done, B)
            attention(Lq[0], "A0")
            feed_forward(0)
            pe.wait_ge(f_x, B)
            l1_coefficients()
            rope_tables()
            l1_denominators()
            pe.wait_ge(rot_out, 1)
            l1_weight()
            l1_attention()
            pe.wait_ge(a_x, B)
            pe.wait_ge(we_done, C)
            feed_forward(1)
            pe.wait_ge(f_x, 2 * B)
            pe.wait_ge(ln_done, LNT["A2"] + B)
            attention(Lq[1], "A2")
            feed_forward(2)
            pe.wait_ge(f_x, 3 * B)
            pe.wait_ge(ln_done, LNT["A3"] + B)
            attention(Lq[2], "A3")
            feed_forward(3)

        @block.vector
        def _(v):
            links = [0]

            def link(ins):
                links[0] += 1
                ins.then_inc(chain, 1)
                v.wait_ge(chain, links[0])

            def norm_stats(phase, b):
                n = LN[phase] + b
                link(v.bn_stats(stats[:, b % 2], x[:, b]))
                link(v.bn_aggr(mv[:, b % 2], stats[:, b % 2]))
                if n >= 2:
                    v.wait_ge(ln_rstd, n - 1)
                v.tensor_scalar(ve[:, b % 2:b % 2 + 1], mv[:, b % 2, 1:2], LN_EPS, None, ALU.add).then_inc(ln_var, 1)

            def norm_rows(phase, b):
                n = LN[phase] + b
                v.wait_ge(ln_rstd, n + 1)
                if phase != "A1" and b >= 2:
                    v.wait_ge(ln_t, LNT[phase] + b - 1)
                if phase == "A1" and b >= 2:
                    v.wait_ge(a_exp, b - 1)
                v.tensor_scalar(xn[:, b % 2], x[:, b], mv[:, b % 2, 0:1], rstd[:, b % 2:b % 2 + 1],
                                ALU.subtract, ALU.mult).then_inc(ln_xn, 1)

            def norm_tail(phase, b):
                n = LNT[phase] + b
                v.wait_ge(ln_head, n + 1)
                cols = slice(b * P, (b + 1) * P)
                v.tensor_tensor(xt_lo[:, :, cols], ps[:, b % 2, :].rearrange("p (c t) -> p c t", c=C),
                                xt_hi[:, :, cols], ALU.subtract).then_inc(ln_done, 1)

            def norm_step(phase, s):
                if 0 <= s < B:
                    norm_stats(phase, s)
                if 1 <= s <= B:
                    norm_rows(phase, s - 1)
                if 2 <= s < B + 2:
                    norm_tail(phase, s - 2)

            def attention(L, phase):
                hd, after = L.hd, "F" + phase[1]

                def evacuate(b, k, i, when=NOW):
                    kind, n = L.fill[b][k]
                    half = L.half[b]
                    batches = slice(half * HALF, (half + 1) * HALF)
                    t, bank = L.tile(i, b, k, when)
                    if kind == "W":
                        return
                    if kind == "V":
                        v.wait_ge(L.s_v_head, L.index("V", i, b, k, when) + 1)
                        v.tensor_tensor(L.v_lo[:, batches, n],
                                        ps[:, bank, 0:HALF * hd].rearrange("p (b d) -> p b d", b=HALF),
                                        L.v_hi[:, batches, n], ALU.subtract).then_inc(L.s_v, 1)
                        return
                    m = L.index("KQ", i, b, k, when)
                    if not L.rope:
                        v.wait_ge(L.s_qk_head, m + 1)
                        if kind == "K":
                            hi, lo = (w[0:hd, batches, n] for w in (L.k_hi, L.k_lo))
                        else:
                            hi, lo = (w[0:hd, n, half * HALF * P:(half + 1) * HALF * P]
                                      .rearrange("p (b t) -> p b t", b=HALF) for w in (L.q_hi, L.q_lo))
                        v.tensor_tensor(lo, ps[0:hd, bank, :].rearrange("p (b t) -> p b t", b=HALF), hi,
                                        ALU.subtract).then_inc(L.s_qk, 1)
                        return
                    v.wait_ge(L.s_proj, t + 1)
                    if when != PROLOGUE or m >= 1:
                        v.wait_ge(L.s_rsum, m)
                    if when != PROLOGUE or m >= 2:
                        v.wait_ge(L.s_qk, m - 1)
                    a = L.index("KQ", 0, b, k, when) % 2
                    hp = P // 2
                    view = lambda ap: ap.rearrange("p (b t) -> p b t", b=HALF)
                    if L.name == "L2":
                        tok = slice(half * 512, (half + 1) * 512)
                        cos, sin = view(cos2[:, tok]), view(sin2[:, tok])
                    else:
                        cos, sin = (rot3[:, j:j + 1, :].to_broadcast([P, HALF, P]) for j in range(2))
                    v.tensor_tensor(view(rope_a[:, a]), view(ps[:, bank, :]), cos, ALU.mult)
                    v.tensor_tensor(view(rope_b[0:hp]), view(ps[hp:P, bank, :]), sin[0:hp], ALU.mult)
                    v.tensor_tensor(view(rope_b[hp:P]), view(ps[0:hp, bank, :]), sin[hp:P],
                                    ALU.mult).then_inc(L.s_rope, 1)

                def row_max(b, i):
                    bank = S_BANK + (b % 2 if L.sources == 1 else 0)
                    v.wait_ge(L.s_s, B * i + b + 1)
                    if L.rope:
                        v.sem_inc(L.s_seen, 1)
                    sc = ps[:, bank:bank + L.sources, :].rearrange("p n (g k) -> p (n g) k", k=L.keys)
                    if L.rope:
                        which = 0 if L.name == "L2" else 1
                        m = mask2[:, b:b + 1, :] if L.name == "L2" else mask3[:, 0:1, :]
                        v.copy_predicated(sc, m.to_broadcast([P, GH, P]),
                                          fill[:, which:which + 1].unsqueeze(2).to_broadcast([P, GH, P])
                                          ).then_inc(L.s_smask, 1)
                        v.wait_ge(L.s_smask, B * i + b + 1)
                    v.tensor_reduce(negmax[:, b % 2], sc, X_AXIS, ALU.max, negate=True).then_inc(L.s_smax, 1)
                    v.wait_ge(L.s_smax, B * i + b + 1)
                    v.tensor_scalar(nbias[:, b % 2], negmax[:, b % 2], L.scale, None, ALU.mult).then_inc(L.s_nb, 1)

                def row_sum(b, i):
                    v.wait_ge(L.s_e, B * i + b + 1 + (2 // L.sources))
                    v.reciprocal(rsums[:, b % 2], sums[:, b % 2]).then_inc(L.s_rs, 1)

                def pt_tail(b, i):
                    v.wait_ge(L.s_pt_head, B * i + b + 1)
                    v.tensor_tensor(L.pt_lo[:], ps[:, T_BANK:T_BANK + L.sources, :], L.pt_hi[:],
                                    ALU.subtract).then_inc(L.s_pt, 1)

                def ot_tail(b, i):
                    v.wait_ge(L.s_o_head, B * i + b + 1)
                    v.tensor_tensor(ot_lo[0:hd], ps[0:hd, O_BANK, :], ot_hi[0:hd], ALU.subtract).then_inc(L.s_ot, 1)

                def residual(b, i):
                    v.wait_ge(L.s_y, B * i + b + 1)
                    v.scalar_tensor_tensor(out=x[:, b], in0=ps[:, Y_BANK, :], scalar=tg[:, L.gate:L.gate + 1],
                                           in1=x[:, b], op0=ALU.mult, op1=ALU.add).then_inc(L.s_x, 1)

                def group(i, last):
                    for b in range(B):
                        if b == 1:
                            pt_tail(0, i)
                        if last and b == 3:
                            evacuate(b - 1, len(L.fill[b - 1]) - 1, i)
                        row_max(b, i)
                        if b >= 2:
                            pt_tail(b - 1, i)
                        if b >= 1 and (not last or b < 3):
                            evacuate(b - 1, len(L.fill[b - 1]) - 1, i)
                        if b >= 2:
                            residual(b - 2, i)
                        row_sum(b, i)
                        if b >= 1:
                            ot_tail(b - 1, i)
                        if b < 3 or (not last and b < B - 1):
                            for k in range(len(L.fill[b]) - 1):
                                evacuate(b, k, i)
                        if last and b >= 3:
                            v.wait_ge(L.s_x, B * i + b - 1)
                            norm_step(after, b - 3)
                    pt_tail(B - 1, i)
                    if not last and L.rope:
                        evacuate(B - 1, 0, i)
                    residual(B - 2, i)
                    ot_tail(B - 1, i)
                    if not last and not L.rope:
                        evacuate(B - 1, 0, i)
                    if not last:
                        evacuate(B - 1, 1, i)
                    residual(B - 1, i)

                v.sem_inc(L.s_x, 1)
                n = 0
                for b in range(3, 8):
                    for k in range(len(L.fill[b])):
                        n += 1
                        if phase == "A0":
                            l1_keys(n)
                        evacuate(b, k, 0, PROLOGUE)
                with v.Fori(0, L.groups - 1) as i:
                    group(i, False)
                group(L.groups - 1, True)
                v.wait_ge(L.s_x, B * L.groups + 1)

            def top2_gate(f, b):
                er, bank = FF[f]["er"], 2 + b % 2
                m = FM[f] + b
                logits = ps[:, bank, er:er + NE]
                bc = lambda col: col.to_broadcast([P, NE])
                e = gt[:, 0]
                v.wait_ge(f_h, m + 1)
                v.tensor_reduce(thr[:, 0:1], logits, X_AXIS, ALU.max, negate=True).then_inc(f_nmax, 1)
                v.wait_ge(f_exp, m + 1)
                link(v.tensor_reduce(gt[:, 1, 0:1], e, X_AXIS, ALU.max))
                link(v.scalar_tensor_tensor(out=gt[:, 2], in0=e, scalar=gt[:, 1, 0:1], in1=iota8,
                                            op0=ALU.is_ge, op1=ALU.mult))
                link(v.tensor_reduce(gt[:, 3, 0:1], gt[:, 2], X_AXIS, ALU.max))
                link(v.tensor_scalar(gt[:, 4], gt[:, 2], gt[:, 3, 0:1], None, ALU.is_equal))
                link(v.scalar_tensor_tensor(out=gt[:, 5], in0=gt[:, 4], scalar=-2.0, in1=e,
                                            op0=ALU.mult, op1=ALU.add))
                link(v.tensor_reduce(gt[:, 6, 0:1], gt[:, 5], X_AXIS, ALU.max))
                link(v.scalar_tensor_tensor(out=gt[:, 7], in0=gt[:, 5], scalar=gt[:, 6, 0:1], in1=iota8,
                                            op0=ALU.is_ge, op1=ALU.mult))
                link(v.tensor_reduce(gt[:, 8, 0:1], gt[:, 7], X_AXIS, ALU.max))
                link(v.scalar_tensor_tensor(out=gt[:, 9], in0=gt[:, 7], scalar=gt[:, 8, 0:1], in1=gt[:, 4],
                                            op0=ALU.is_equal, op1=ALU.add))
                link(v.tensor_tensor(gt[:, 10], gt[:, 9], e, ALU.mult))
                link(v.tensor_reduce(gt[:, 11, 0:1], gt[:, 10], X_AXIS, ALU.add))
                link(v.reciprocal(gt[:, 12, 0:1], gt[:, 11, 0:1]))
                link(v.tensor_scalar(gt[:, 13], gt[:, 10], gt[:, 12, 0:1], 2.0, ALU.mult, ALU.mult))
                weigh(f, b)

            def threshold_gate(f, b):
                er, bank = FF[f]["er"], 2 + b % 2
                m = FM[f] + b
                v.wait_ge(f_h, m + 1)
                v.tensor_reduce(thr[:, 0:1], ps[:, bank, er:er + NE], X_AXIS, ALU.max, negate=True).then_inc(f_nmax, 1)
                v.wait_ge(f_exp, m + 1)
                v.reciprocal(gt[:, 1, 0:1], thr[:, 1:2])
                link(v.tensor_scalar(gt[:, 2, 0:1], thr[:, 2:3], 1.0, None, ALU.add))
                link(v.reciprocal(gt[:, 3, 0:1], gt[:, 2, 0:1]))
                link(v.tensor_scalar(gt[:, 4, 0:1], gt[:, 3, 0:1], 0.125, None, ALU.mult))
                link(v.tensor_scalar(gt[:, 5], gt[:, 0], gt[:, 1, 0:1], gt[:, 4, 0:1], ALU.mult, ALU.subtract))
                link(v.tensor_scalar(gt[:, 6], gt[:, 5], 0.0, None, ALU.max))
                link(v.tensor_reduce(gt[:, 7, 0:1], gt[:, 6], X_AXIS, ALU.add))
                link(v.scalar_tensor_tensor(out=gt[:, 8, 0:1], in0=gt[:, 7, 0:1], scalar=0.0, in1=gt[:, 7, 0:1],
                                            op0=ALU.is_equal, op1=ALU.add))
                link(v.reciprocal(gt[:, 9, 0:1], gt[:, 8, 0:1]))
                link(v.tensor_scalar(gt[:, 13], gt[:, 6], gt[:, 9, 0:1], 2.0, ALU.mult, ALU.mult))
                weigh(f, b)

            def weigh(f, b):
                er, bank, m = FF[f]["er"], 2 + b % 2, FM[f] + b
                if m >= 2:
                    v.wait_ge(f_t, m - 1)
                v.tensor_tensor(hw[:, b % 2, 0:er].rearrange("p (e r) -> p e r", e=NE),
                                ps[:, bank, 0:er].rearrange("p (e r) -> p e r", e=NE),
                                gt[:, 13].unsqueeze(2).to_broadcast([P, NE, er // NE]), ALU.mult).then_inc(f_hw, 1)

            def feed_forward(f):
                F, phase, gate = FF[f], f"F{f}", 2 * f + 1
                er = F["er"]
                if f >= 1:
                    v.wait_ge(b_in, 16 * (FB[f] + 1))
                    v.tensor_scalar(bias[:], bias[:], tg[:, gate:gate + 1], None, ALU.mult).then_inc(b_tg, 1)
                for s in range(FF_START[f], B + 12 if f in FF_NEXT else B + 8):
                    norm_step(phase, s)
                    if er and 6 <= s < B + 6:
                        (threshold_gate if f == 3 else top2_gate)(f, s - 6)
                    if er and 7 <= s < B + 7:
                        b = s - 7
                        v.wait_ge(f_thead, FM[f] + b + 1)
                        v.tensor_tensor(hwt_lo[0:er], ps[0:er, 2 + b % 2, 256:384], hwt_hi[0:er],
                                        ALU.subtract).then_inc(f_tdone, 1)
                    if 8 <= s < B + 8:
                        b = s - 8
                        v.wait_ge(f_y, FN[f] + b + 1)
                        if f >= 1:
                            v.wait_ge(b_x, FB[f] * B + b + 1)
                        v.scalar_tensor_tensor(out=x[:, b], in0=ps[:, 4 + b % 4, :], scalar=tg[:, gate:gate + 1],
                                               in1=x[:, b], op0=ALU.mult, op1=ALU.add).then_inc(f_x, 1)
                    if f in FF_NEXT and s >= 9:
                        if s - 9 < B:
                            v.wait_ge(f_x, FN[f] + s - 8)
                            norm_stats(FF_NEXT[f], s - 9)
                        if 0 <= s - 10 < B:
                            norm_rows(FF_NEXT[f], s - 10)
                        if 0 <= s - 12 < B:
                            norm_tail(FF_NEXT[f], s - 12)
                v.wait_ge(f_x, FN[f] + B)

            def l1_keys(s):
                if s <= B + 1:
                    if s < B:
                        v.wait_ge(cn_in[s // 4], 64)
                        v.tensor_reduce(negmax[:, s % 2, s // 2:s // 2 + 1], cn_raw[:, s], X_AXIS, ALU.max,
                                        negate=True).then_inc(k_nmax, 1)
                    if 1 <= s <= B:
                        b = s - 1
                        v.wait_ge(k_head, b + 1)
                        v.tensor_tensor(kt_lo[:, b % 2], ps[:, 2 + b % 2, :].rearrange("p (c k) -> p c k", c=C),
                                        kt_hi[:, b % 2], ALU.subtract).then_inc(k_done, 1)
                    if s >= 2:
                        b = s - 2
                        v.wait_ge(k_kv, b + 1)
                        link(v.reciprocal(rsums[:, 0, 0:1], sums[:, b % 2, b // 2:b // 2 + 1]))
                        link(v.scalar_tensor_tensor(out=kvm[:], in0=ps[:, 4 + b % 2, 0:P], scalar=rsums[:, 0, 0:1],
                                                    in1=blk, op0=ALU.mult, op1=ALU.mult))
                        v.tensor_reduce(kc[:, b], kvm[:].rearrange("p (g e) -> p e g", e=16), X_AXIS,
                                        ALU.add).then_inc(k_sum, 1)

            def l1_attention():
                for s in range(B + 2):
                    if s < B:
                        norm_stats("A1", s)
                    if 1 <= s <= B:
                        norm_rows("A1", s - 1)
                    if s >= 2:
                        b = s - 2
                        v.wait_ge(a_head, b + 1)
                        v.tensor_tensor(e_lo[:, b], probs[:, b % 2 * D:(b % 2 + 1) * D], e_hi[:, b],
                                        ALU.subtract).then_inc(a_done, 1)
                v.wait_ge(gk_mm, 1)
                v.tensor_scalar(gk[:], ps[0:40, 0, :], 0.5, None, ALU.mult).then_inc(gk_done, 1)
                v.wait_ge(a_den, 1)
                v.reciprocal(vt[0:B * 8], ps[0:B * 8, 2, :]).then_inc(a_rec, 1)
                for c in range(C):
                    s = raw_ready(v, W_BASE["F1"], c, 0, 0)
                    v.wait_ge(we_mm, c + 1)
                    v.tensor_tensor(raw[:, s, 0:D], ps[:, 4 + c, :], raw[:, s, 0:D], ALU.add).then_inc(we_done, 1)
                v.wait_ge(a_rhead, 1)
                v.tensor_tensor(ot_lo[0:B * 8], vt[0:B * 8], ot_hi[0:B * 8], ALU.subtract).then_inc(a_rdone, 1)
                for b in range(B):
                    v.wait_ge(a_num, b + 1)
                    v.wait_ge(a_copy, b + 1)
                    link(v.tensor_tensor(xn[:, b % 2], ps[:, 2 + b % 2, :], probs[:, b % 2 * D:(b % 2 + 1) * D],
                                         ALU.mult))
                    v.scalar_tensor_tensor(out=x[:, b], in0=xn[:, b % 2], scalar=tg[:, 2:3], in1=x[:, b],
                                           op0=ALU.mult, op1=ALU.add).then_inc(a_x, 1)
                v.wait_ge(a_x, B)

            v.memset(minus_half[:], -0.5)
            v.memset(fill[:, 0:1], -1.0e9 * float(P) ** 0.5)
            v.memset(fill[:, 1:2], -3.4028234e38).then_inc(cst, 1)
            for s in range(B + 2):
                if s < B:
                    v.wait_ge(x_in[s // 2], 32)
                norm_step("A0", s)
            for c in range(C):
                v.wait_ge(ct_head, c + 1)
                v.tensor_tensor(ct_lo[:, c], ct_raw[:, c], ct_hi[:, c], ALU.subtract).then_inc(ct_done, 1)
            v.wait_ge(cst_in, 16)
            l1_keys(0)
            v.wait_ge(g_tanh, 2)
            attention(Lq[0], "A0")
            feed_forward(0)
            l1_attention()
            feed_forward(1)
            v.wait_ge(m_in, 32)
            v.tensor_scalar(mask2[:], mask_in[:], 0.0, None, ALU.is_equal)
            v.tensor_scalar(mask3[:, 0], causal[:], 0.0, None, ALU.is_equal).then_inc(m_done, 1)
            v.wait_ge(m_done, 1)
            attention(Lq[1], "A2")
            feed_forward(2)
            v.wait_ge(rot3_in, 16)
            attention(Lq[2], "A3")
            feed_forward(3)

        @block.scalar
        def _(act):
            def norm_head(phase, b):
                n = LNT[phase] + b
                act.wait_ge(ln_t, n + 1)
                act.copy(xt_hi[:, :, b * P:(b + 1) * P],
                         ps[:, b % 2, :].rearrange("p (c t) -> p c t", c=C)).then_inc(ln_head, 1)

            def weight_head(base, n_static, per_loop, i, dst, cols, parts=P):
                s = raw_ready(act, base, n_static, per_loop, i)
                act.copy(dst, raw[0:parts, s, 0:cols]).then_inc(w_head, 1)

            def attention(L, phase):
                base, hd, after = W_BASE[phase], L.hd, "F" + phase[1]

                def proj_weight(t, i, n_static, per_loop):
                    dst = {0: L.wq_hi[:, 0], 1: L.wkv_hi[:, 0], 2: L.wq_hi[:, 1], 3: L.wkv_hi[:, 1],
                           4: L.wq_hi[:, 2], 5: L.wq_hi[:, 3]}[t]
                    weight_head(base, n_static, per_loop, i, dst.rearrange("p c d -> p (c d)"), C * hd)

                def head(b, k, i, when=NOW):
                    kind, n = L.fill[b][k]
                    half = L.half[b]
                    t, bank = L.tile(i, b, k, when)
                    m, a = L.index("KQ", i, b, k, when), L.index("KQ", 0, b, k, when) % 2
                    if kind == "W":
                        act.wait_ge(L.s_proj, t + 1)
                        act.copy(vt[0:hd], ps[0:hd, bank, :]).then_inc(L.s_w, 1)
                        return
                    if kind == "V":
                        act.wait_ge(L.s_proj, t + 1)
                        act.copy(L.v_hi[:, half * HALF:(half + 1) * HALF, n],
                                 ps[:, bank, 0:HALF * hd].rearrange("p (b d) -> p b d", b=HALF)
                                 ).then_inc(L.s_v_head, 1)
                        return
                    if kind == "K":
                        dst = L.k_hi[0:hd, half * HALF:(half + 1) * HALF, n]
                    else:
                        dst = L.q_hi[0:hd, n, half * HALF * P:(half + 1) * HALF * P].rearrange(
                            "p (b t) -> p b t", b=HALF)
                    if L.rope:
                        act.wait_ge(L.s_rsum, m + 1)
                        src = rope_a[:, a]
                    else:
                        act.wait_ge(L.s_proj, t + 1)
                        src = ps[0:hd, bank, :]
                    act.copy(dst, src.rearrange("p (b t) -> p b t", b=HALF)).then_inc(L.s_qk_head, 1)

                def exps(b, i):
                    bank = S_BANK + (b % 2 if L.sources == 1 else 0)
                    act.wait_ge(L.s_nb, B * i + b + 1)
                    for h in range(GH):
                        at_ = h * L.keys
                        e = act.activation(probs[:, at_:at_ + L.keys],
                                           ps[:, bank + at_ // 512, at_ % 512:at_ % 512 + L.keys], ACT.Exp,
                                           bias=nbias[:, b % 2, h:h + 1], scale=L.scale,
                                           accum_out=sums[:, b % 2, h:h + 1])
                    e.then_inc(L.s_e, 1)

                def pt_head(b, i):
                    act.wait_ge(L.s_t, B * i + b + 1)
                    act.copy(L.pt_hi[:], ps[:, T_BANK:T_BANK + L.sources, :]).then_inc(L.s_pt_head, 1)

                def o_head(b, i):
                    act.wait_ge(L.s_o, B * i + b + 1)
                    act.copy(ot_hi[0:hd], ps[0:hd, O_BANK, :]).then_inc(L.s_o_head, 1)

                def group(i, last):
                    for b in range(B):
                        if b >= 1:
                            pt_head(b - 1, i)
                        late = b == 0 or not last or b <= 3
                        early = (b == 0 or not L.rope or L.fill[(b - 1) % 8][-1][0] == "W" or last and b == 3)
                        if late and early:
                            head((b - 1) % 8, len(L.fill[(b - 1) % 8]) - 1, i, NOW if b else BEFORE)
                        if L.rope and (b == 1 or b == 5 and not last):
                            head(b - 1, 0, i)
                        exps(b, i)
                        if late and not early:
                            head((b - 1) % 8, len(L.fill[(b - 1) % 8]) - 1, i, NOW if b else BEFORE)
                        if b >= 1:
                            o_head(b - 1, i)
                        if b < 3 or (not last and b < B - 1):
                            for k in range(len(L.fill[b]) - 1):
                                if not (L.rope and b % HALF == 0):
                                    head(b, k, i)
                        if b == 0:
                            act.wait_ge(L.s_x, B * i + 1)
                            for h in range(GH):
                                weight_head(base, 6 + h, 10, i, L.wo_hi[0:hd, h], D, hd)
                        elif not last:
                            for t in SPLIT_AT.get(b, []):
                                proj_weight(t, i, 10 + t, 10)
                        if last and b >= 4:
                            if b == 4:
                                act.wait_ge(L.s_proj, L.tiles)
                            weight_head(W_BASE[after], b - 4, 0, 0, wt_hi[:, b - 4], D)
                        if last and b >= 5:
                            norm_head(after, b - 5)
                    pt_head(B - 1, i)
                    o_head(B - 1, i)
                    if not last:
                        head(B - 1, 0, i)

                act.sem_inc(L.s_e, 2 // L.sources)
                for t in range(6):
                    proj_weight(t, 0, t, 0)
                if phase == "A0":
                    l1_keys(0)
                n = 0
                for b in range(3, 8):
                    for k in range(len(L.fill[b])):
                        if (b, k) != (7, len(L.fill[7]) - 1):
                            n += 1
                            if phase == "A0":
                                l1_keys(n)
                            head(b, k, 0, PROLOGUE)
                with act.Fori(0, L.groups - 1) as i:
                    group(i, False)
                group(L.groups - 1, True)

            def ff_weights(f):
                F, base = FF[f], W_BASE[f"F{f}"]
                if F["er"]:
                    weight_head(base, C, 0, 0, F["ag_hi"][:].rearrange("p c n -> p (c n)"), C * F["cols"])
                    weight_head(base, C + 1, 0, 0, F["lb_hi"][0:F["er"]], D, F["er"])

            def feed_forward(f):
                F, phase = FF[f], f"F{f}"
                er = F["er"]
                for s in range(FF_START[f], B + 12 if f in FF_NEXT else B + 8):
                    if 2 <= s < B + 2:
                        norm_head(phase, s - 2)
                    if er and 6 <= s < B + 6:
                        b = s - 6
                        act.wait_ge(f_nmax, FM[f] + b + 1)
                        e = act.activation(gt[:, 0], ps[:, 2 + b % 2, er:er + NE], ACT.Exp, bias=thr[:, 0:1],
                                           accum_out=thr[:, 1:2])
                        if f == 3:
                            e = act.activation(thr[:, 2:3], ps[:, 2 + b % 2, er + NE:er + NE + 1], ACT.Exp,
                                               bias=thr[:, 3:4], scale=-1.0)
                        e.then_inc(f_exp, 1)
                    if er and 7 <= s < B + 7:
                        b = s - 7
                        act.wait_ge(f_t, FM[f] + b + 1)
                        act.copy(hwt_hi[0:er], ps[0:er, 2 + b % 2, 256:384]).then_inc(f_thead, 1)
                    if f in FF_NEXT and 12 <= s:
                        norm_head(FF_NEXT[f], s - 12)

            def l1_keys(s):
                if s <= B:
                    if s < B:
                        act.wait_ge(k_nmax, s + 1)
                        if s >= 2:
                            act.wait_ge(k_t, s - 1)
                        act.activation(probs[:, s % 2 * D:(s % 2 + 1) * D], cn_raw[:, s], ACT.Exp,
                                       bias=negmax[:, s % 2, s // 2:s // 2 + 1],
                                       accum_out=sums[:, s % 2, s // 2:s // 2 + 1]).then_inc(k_exp, 1)
                    if s >= 1:
                        b = s - 1
                        act.wait_ge(k_t, b + 1)
                        if b >= 2:
                            act.wait_ge(k_kv, b - 1)
                        act.copy(kt_hi[:, b % 2], ps[:, 2 + b % 2, :].rearrange("p (c k) -> p c k", c=C)
                                 ).then_inc(k_head, 1)

            def l1_attention():
                act.wait_ge(tab_in, 16)
                act.copy(tab_hi[:], tab_raw[:]).then_inc(tab_head, 1)
                act.wait_ge(sel_dma, 32)
                act.copy(sel[:], sel_in[:]).then_inc(sel_done, 1)
                act.copy(spread[:], spread_in[:]).then_inc(sel_done, 1)
                for b in range(B):
                    act.wait_ge(ln_xn, LN["A1"] + b + 1)
                    if b >= 2:
                        act.wait_ge(a_done, b - 1)
                    act.activation(probs[:, b % 2 * D:(b % 2 + 1) * D], xn[:, b % 2], ACT.Exp).then_inc(a_exp, 1)
                    act.wait_ge(a_exp, b + 1)
                    act.copy(e_hi[:, b], probs[:, b % 2 * D:(b % 2 + 1) * D]).then_inc(a_head, 1)
                act.wait_ge(k_kvs, 1)
                act.copy(kvs_hi[:], kvs[:]).then_inc(k_kvhead, 1)
                act.wait_ge(oh_mm, C)
                act.copy(cos2[:], ps[:, 4:6, :].rearrange("p a b -> p (a b)"))
                act.copy(sin2[:], ps[:, 6:8, :].rearrange("p a b -> p (a b)")).then_inc(rot_out, 1)
                act.wait_ge(a_rec, 1)
                act.copy(ot_hi[0:B * 8], vt[0:B * 8]).then_inc(a_rhead, 1)
                for b in range(B):
                    act.wait_ge(a_bc, b + 1)
                    if b >= 2:
                        act.wait_ge(a_x, b - 1)
                    act.copy(probs[:, b % 2 * D:(b % 2 + 1) * D], ps[:, b % 2, :]).then_inc(a_copy, 1)
                    if 2 <= b < 2 + C:
                        act.wait_ge(we_done, b - 1)
                        weight_head(W_BASE["F1"], b - 2, 0, 0, wt_hi[:, b - 2], D)

            act.wait_ge(g_in, 32)
            act.activation(tg[:], gates[:], ACT.Tanh).then_inc(g_tanh, 1)
            act.mul(thr[:, 3:4], bthr[:], -1.0).then_inc(g_tanh, 1)
            act.wait_ge(g_tanh, 2)
            for b in range(B):
                norm_head("A0", b)
            act.wait_ge(ct_in, 16 * C)
            for c in range(C):
                act.copy(ct_hi[:, c], ct_raw[:, c]).then_inc(ct_head, 1)
            attention(Lq[0], "A0")
            ff_weights(0)
            feed_forward(0)
            l1_attention()
            ff_weights(1)
            feed_forward(1)
            attention(Lq[1], "A2")
            ff_weights(2)
            feed_forward(2)
            attention(Lq[2], "A3")
            ff_weights(3)
            feed_forward(3)

        @block.gpsimd
        def _(gp):
            def norm_rstd(phase, b):
                n = LN[phase] + b
                gp.wait_ge(ln_var, n + 1)
                if n >= 2:
                    gp.wait_ge(ln_xn, n - 1)
                gp.tensor_tensor(rstd[:, b % 2:b % 2 + 1], ve[:, b % 2:b % 2 + 1], minus_half[:],
                                 ALU.pow).then_inc(ln_rstd, 1)

            def weight_tail(base, n_static, per_loop, i, lo, hi, cols, parts=P):
                k = base + n_static
                gp.wait_ge(w_head, k + 1 + per_loop * i)
                gp.tensor_tensor(lo, raw[0:parts, k % RAW, 0:cols], hi, ALU.subtract).then_inc(w_done, 1)

            def attention(L, phase):
                base, hd, after = W_BASE[phase], L.hd, "F" + phase[1]

                def proj_weight(t, i, n_static, per_loop):
                    lo, hi = {0: (L.wq_lo[:, 0], L.wq_hi[:, 0]), 1: (L.wkv_lo[:, 0], L.wkv_hi[:, 0]),
                              2: (L.wq_lo[:, 1], L.wq_hi[:, 1]), 3: (L.wkv_lo[:, 1], L.wkv_hi[:, 1]),
                              4: (L.wq_lo[:, 2], L.wq_hi[:, 2]), 5: (L.wq_lo[:, 3], L.wq_hi[:, 3])}[t]
                    weight_tail(base, n_static, per_loop, i, lo.rearrange("p c d -> p (c d)"),
                                hi.rearrange("p c d -> p (c d)"), C * hd)

                def wo_tail(h, i):
                    weight_tail(base, 6 + h, 10, i, L.wo_lo[0:hd, h], L.wo_hi[0:hd, h], D, hd)

                def rotated(b, k, i, when):
                    return L.index("KQ", i, b, k, when), L.index("KQ", 0, b, k, when) % 2

                def add_up(b, k, i, when=NOW):
                    m, a = rotated(b, k, i, when)
                    gp.wait_ge(L.s_rope, m + 1)
                    gp.tensor_tensor(rope_a[:, a], rope_a[:, a], rope_b[:], ALU.add).then_inc(L.s_rsum, 1)

                def tail(b, k, i, when=NOW):
                    m, a = rotated(b, k, i, when)
                    kind, n = L.fill[b][k]
                    half = L.half[b]
                    if kind == "K":
                        lo, hi = (w[:, half * HALF:(half + 1) * HALF, n].rearrange("p b t -> p (b t)")
                                  for w in (L.k_lo, L.k_hi))
                    else:
                        lo, hi = (w[:, n, half * HALF * P:(half + 1) * HALF * P] for w in (L.q_lo, L.q_hi))
                    gp.wait_ge(L.s_qk_head, m + 1)
                    gp.tensor_tensor(lo, rope_a[:, a], hi, ALU.subtract).then_inc(L.s_qk, 1)

                def normalise(b, i):
                    gp.wait_ge(L.s_rs, B * i + b + 1)
                    pv = probs[:, 0:GH * L.keys].rearrange("p (h k) -> p h k", h=GH)
                    gp.tensor_tensor(pv, pv, rsums[:, b % 2].unsqueeze(2).to_broadcast([P, GH, L.keys]),
                                     ALU.mult).then_inc(L.s_p, 1)

                def group(i, last):
                    for b in range(B):
                        late = L.rope and (b == 0 or not last or b <= 3)
                        pb = (b - 1) % 8
                        late = late and L.fill[pb][-1][0] != "W"
                        if late:
                            add_up(pb, len(L.fill[pb]) - 1, i, NOW if b else BEFORE)
                        if late and (b == 0 or last and b == 3):
                            tail(pb, len(L.fill[pb]) - 1, i, NOW if b else BEFORE)
                        normalise(b, i)
                        if b == 1:
                            wo_tail(GH - 1, i)
                        if L.rope and (b == 1 or b == 5 and not last):
                            tail(b - 1, 0, i)
                        if late and b >= 1 and not (last and b == 3):
                            tail(pb, len(L.fill[pb]) - 1, i)
                        if L.rope and (not last or b < 3):
                            for k, (kind, _) in enumerate(L.fill[b][:-1]):
                                if kind in "KQ":
                                    add_up(b, k, i)
                                    if b % HALF:
                                        tail(b, k, i)
                        if b == 0:
                            for h in range(GH - 1):
                                wo_tail(h, i)
                        elif not last:
                            for t in SPLIT_AT.get(b, []):
                                proj_weight(t, i, 10 + t, 10)
                        if last and b >= 4:
                            weight_tail(W_BASE[after], b - 4, 0, 0, wt_lo[:, b - 4], wt_hi[:, b - 4], D)
                        if last and b >= 3:
                            norm_rstd(after, b - 3)

                for t in range(6):
                    proj_weight(t, 0, t, 0)
                if L.rope:
                    for b in range(3, 8):
                        for k, (kind, _) in enumerate(L.fill[b]):
                            if kind in "KQ" and (b, k) != (7, len(L.fill[7]) - 1):
                                add_up(b, k, 0, PROLOGUE)
                                tail(b, k, 0, PROLOGUE)
                with gp.Fori(0, L.groups - 1) as i:
                    group(i, False)
                group(L.groups - 1, True)

            def ff_weights(f):
                F, base = FF[f], W_BASE[f"F{f}"]
                if f == 1:
                    for c in range(C):
                        weight_tail(base, c, 0, 0, wt_lo[:, c], wt_hi[:, c], D)
                if F["er"]:
                    weight_tail(base, C, 0, 0, F["ag_lo"][:].rearrange("p c n -> p (c n)"),
                                F["ag_hi"][:].rearrange("p c n -> p (c n)"), C * F["cols"])
                    weight_tail(base, C + 1, 0, 0, F["lb_lo"][0:F["er"]], F["lb_hi"][0:F["er"]], D, F["er"])

            def feed_forward(f):
                phase = f"F{f}"
                for b in range(min(FF_START[f], B), B):
                    norm_rstd(phase, b)
                    if f >= 1 and b >= 1:
                        for earlier in (range(b) if b == FF_START[f] else (b - 1,)):
                            add_bias(f, earlier)
                if f >= 1:
                    add_bias(f, B - 1)
                if f in FF_NEXT:
                    for b in range(B):
                        norm_rstd(FF_NEXT[f], b)

            def add_bias(f, b):
                if b == 0:
                    gp.wait_ge(b_tg, FB[f] + 1)
                gp.wait_ge(ln_xn, LN[f"F{f}"] + b + 1)
                gp.tensor_tensor(x[:, b], x[:, b], bias[:], ALU.add).then_inc(b_x, 1)

            def own(ins):
                links[0] += 1
                ins.then_inc(pchain, 1)
                gp.wait_ge(pchain, links[0])

            links = [0]

            def l1_preparations():
                gp.wait_ge(pos_in, 16)
                own(gp.tensor_copy(pos_f[:], pos_i[:]))
                own(gp.tensor_scalar(pos_n[:], pos_f[:], 0.0, float(C * P), ALU.is_lt, ALU.mult))
                own(gp.tensor_tensor(pos_f[:], pos_f[:], pos_n[:], ALU.add))
                own(gp.tensor_scalar(pos_f[:], pos_f[:], 0.0, float(C * P - 1), ALU.max, ALU.min))
                for c in range(C):
                    gp.tensor_scalar(onehot[c][:], pos_f[:], pidx[:, c:c + 1], None,
                                     ALU.is_equal).then_inc(oh, 1)
                gp.wait_ge(four_in, 64)
                own(gp.tensor_copy(cm_f[:], cm_in[:]))
                own(gp.tensor_tensor(cf_in[:], cf_in[:], cm_f[:], ALU.mult))
                own(gp.tensor_tensor(ws[:], cf_in[:, :, 0], cf_in[:, :, 1], ALU.add))
                gp.tensor_tensor(ws[:], ws[:], cf_in[:, :, 2], ALU.add).then_inc(ws_done, 1)
                for b in range(B):
                    ins = gp.tensor_tensor(kvs[:, b].rearrange("p (g e) -> p g e", e=16),
                                           kc[:, b:b + 1].to_broadcast([P, P // 16, 16]),
                                           blk.rearrange("p (g e) -> p g e", e=16), ALU.mult)
                ins.then_inc(k_kvs, 1)
                gp.wait_ge(tab_head, 1)
                gp.tensor_tensor(tab_lo[:], tab_raw[:], tab_hi[:], ALU.subtract).then_inc(tab_done, 1)

            gp.wait_ge(cst, 1)
            for b in range(B):
                norm_rstd("A0", b)
            attention(Lq[0], "A0")
            ff_weights(0)
            feed_forward(0)
            l1_preparations()
            for b in range(B):
                norm_rstd("A1", b)
            gp.wait_ge(k_kvhead, 1)
            gp.tensor_tensor(kvs_lo[:], kvs[:], kvs_hi[:], ALU.subtract).then_inc(k_kvdone, 1)
            ff_weights(1)
            feed_forward(1)
            attention(Lq[1], "A2")
            ff_weights(2)
            feed_forward(2)
            attention(Lq[2], "A3")
            ff_weights(3)
            feed_forward(3)


def shape_constants():
    import numpy as _np
    f = _np.float32
    consts = _np.zeros((P, 2 * P + NE + C), f)
    consts[:, 0:P] = _np.eye(P)
    consts[:, P:2 * P] = _np.kron(_np.eye(P // 16), _np.ones((16, 16)))
    consts[:, 2 * P:2 * P + NE] = _np.arange(NE, 0, -1)
    consts[:, 2 * P + NE:] = _np.arange(P)[:, None] + P * _np.arange(C)[None, :]
    inv = (f(1.0) / _np.power(f(10000.0), _np.arange(0, P, 2, dtype=f) / f(P))).astype(f)
    ang = (_np.arange(C * P, dtype=f)[:, None] * inv[None, :]).astype(f)
    cos = _np.concatenate([_np.cos(ang), _np.cos(ang)], 1).astype(f)
    sin = _np.concatenate([-_np.sin(ang), _np.sin(ang)], 1).astype(f)
    rope2 = _np.stack([cos, sin], 1).reshape(C, P, 2, P).transpose(1, 0, 2, 3)
    rope3 = _np.stack([cos[:P].T, sin[:P].T], 1)
    n = D
    t = _np.arange(n)
    four = _np.zeros((n, n))
    four[0] = 1.0 / _np.sqrt(n)
    four[n - 1] = _np.where(t % 2 == 0, 1.0, -1.0) / _np.sqrt(n)
    for k in range(1, (n - 1) // 2 + 1):
        four[2 * k - 1] = _np.sqrt(2.0 / n) * _np.cos(2 * _np.pi * k * t / n)
        four[2 * k] = _np.sqrt(2.0 / n) * _np.sin(2 * _np.pi * k * t / n)
    fourier = four.astype(f).reshape(C, P, n).transpose(1, 0, 2)
    causal = _np.tril(_np.ones((P, P), f))
    row = 8 * _np.arange(B)[None, :, None] + (_np.arange(P) // 16)[:, None, None]
    sel = (row == _np.arange(B * 8)[None, None, :]).astype(f)
    spread = sel.transpose(2, 1, 0)
    return dict(sel=sel, spread=spread, consts=consts, rope2=rope2, rope3=rope3, fourier=fourier, causal=causal)


def kernel(**inputs):
    import numpy as _np
    import concourse.bacc as _bacc
    from concourse import mybir as _mybir
    from concourse.bass_utils import run_bass_kernel_spmd as _run

    a = {k: _np.asarray(v) for k, v in inputs.items()}

    def proj_tiles(wq, wk, wv, hd, groups):
        q = wq.reshape(C, P, groups, GH, hd).transpose(2, 3, 1, 0, 4).reshape(groups, GH, P, C * hd)
        k = wk.reshape(C, P, groups, hd).transpose(2, 1, 0, 3).reshape(groups, 1, P, C * hd)
        v = wv.reshape(C, P, groups, hd).transpose(2, 1, 0, 3).reshape(groups, 1, P, C * hd)
        return _np.concatenate([q[:, 0:1], k, q[:, 1:2], v, q[:, 2:4]], 1)

    def chunked(w):
        return w.reshape(C, P, -1).transpose(1, 0, 2).reshape(P, -1)

    arr = dict(shape_constants())
    arr["x"] = a["x"]
    arr["ctx"] = a["ctx_4096"]
    arr["ctx_t"] = a["ctx_4096"].reshape(T, C, P).transpose(1, 2, 0)
    arr["pos"] = a["pos_BxS2"].reshape(1, T)
    arr["mask"] = a["mask_BxSxS2_ik0"].transpose(1, 0, 2)
    arr["gates"] = _np.stack([a["g_xattn"], a["g_ffn"]], 1).reshape(1, 8)
    arr["b_thr"] = a["L3_ffn_b_thr"].reshape(1, 1)
    arr["L0_proj"] = proj_tiles(a["L0_xattn_Wq"].T, a["L0_xattn_Wk"].T, a["L0_xattn_Wv"].T, 96, 4)
    arr["L0_out"] = a["L0_xattn_Wo"].T.reshape(4, GH, 96, D)
    arr["L2_proj"] = proj_tiles(a["L2_xattn_Wq"], a["L2_xattn_Wk"], a["L2_xattn_Wv"], 128, 8)
    arr["L2_out"] = a["L2_xattn_Wo"].reshape(8, GH, 128, D)
    arr["L3_proj"] = proj_tiles(a["L3_xattn_Wq"].T, a["L3_xattn_Wk"].T, a["L3_xattn_Wv"].T, 128, 8)
    arr["L3_out"] = a["L3_xattn_Wd"].T.reshape(8, GH, 128, D)
    for f in range(4):
        arr[f"F{f}_w"] = a[f"L{f}_ffn_W_base"].T.reshape(C, P, D)
        if f >= 1:
            arr[f"F{f}_bias"] = a[f"L{f}_ffn_b_base"].reshape(1, D)
    lora = {0: ("L0_ffn_A", "L0_ffn_gate_W", "L0_ffn_B"), 2: ("L2_ffn_lora_A", "L2_ffn_W_router", "L2_ffn_lora_B"),
            3: ("L3_ffn_A_w", "L3_ffn_W_gate", "L3_ffn_B_w")}
    for f, (la, lg, lb) in lora.items():
        cols = [a[la].reshape(-1, D).T, a[lg].T]
        if f == 3:
            cols += [a["L3_ffn_W_thr"].reshape(D, 1)] * 2
        arr[f"F{f}_ag"] = chunked(_np.concatenate(cols, 1))
        arr[f"F{f}_b"] = a[lb].transpose(0, 2, 1).reshape(-1, D)
    rows = lambda w: w.reshape(3, C, P, -1).transpose(2, 1, 0, 3)
    arr["F1_coef"] = _np.concatenate([rows(a["L1_ffn_coefs0"]), rows(a["L1_ffn_coefs1"])], 3)
    arr["F1_mask"] = _np.concatenate([rows(a["L1_ffn_mask0"]), rows(a["L1_ffn_mask1"])], 3).astype(_np.int32)
    arr["F1_enc"] = _np.concatenate([a["L1_ffn_enc0"], a["L1_ffn_enc1"]], 0)

    nc = _bacc.Bacc("TRN2", target_bir_lowering=False, num_devices=1, dynamic_dma_scratch_size=256)
    feed, aps = {}, {}
    for name, w in arr.items():
        w = _np.ascontiguousarray(w)
        feed[f"in_{name}"] = w
        aps[name] = nc.dram_tensor(f"in_{name}", w.shape, _mybir.dt.from_np(w.dtype), kind="ExternalInput").ap()
    out = nc.dram_tensor("out_0", (B, P, D), _mybir.dt.float32, kind="ExternalOutput").ap()
    build(nc, aps, out)
    r = _run(nc, [feed], core_ids=[0])
    return r.results[0]["out_0"]
```
